# Optimizing a Trainium2 kernel written in Bass

```python
import numpy as np
import jax
import jax.numpy as jnp

def _softmax(x, axis=-1):
    return jax.nn.softmax(x, axis=axis)

def _gelu(x):
    return jax.nn.gelu(x, approximate=True)

def _silu(x):
    return jax.nn.silu(x)

def _sigmoid(x):
    return jax.nn.sigmoid(x)

def _layernorm(x, axis=-1, eps=1e-05):
    m = jnp.mean(x, axis=axis, keepdims=True)
    v = jnp.var(x, axis=axis, keepdims=True)
    return (x - m) / jnp.sqrt(v + eps)

def _scatter_add(tgt, idx, src, axis=0):
    return tgt.at[idx].add(src)

def _segment_sum(src, seg, n):
    return jax.ops.segment_sum(src, seg, n)
kernel_name = 'mk_decoder_postln_d1_seqx_r8_7f6edc'

def setup_inputs(seed: int=0):
    np.random.seed(seed)
    _w = jnp.asarray

    def _rec_inputs():
        import jax
        import jax.numpy as jnp
        _rk = jax.random.key(seed)
        x = -0.0002928 + 1 * jax.random.normal(jax.random.fold_in(_rk, 1), (8, 256, 128), jnp.float32)
        _lenS = 256 - jax.random.randint(jax.random.fold_in(_rk, 7), (8,), 0, max(1, 256 // 4) + 1, jnp.int32)
        _lenS2 = 512 - jax.random.randint(jax.random.fold_in(_rk, 8), (8,), 0, max(1, 512 // 4) + 1, jnp.int32)
        _ctx_1024P = jax.random.normal(jax.random.fold_in(_rk, 11), (8, 16, 128), jnp.float32)
        _ctx_1024c = jax.random.dirichlet(jax.random.fold_in(_rk, 511), 0.3 * jnp.ones((16,), jnp.float32), (8, 512))
        _ctx_1024t = jnp.einsum('bsk,bkd->bsd', _ctx_1024c, _ctx_1024P)
        _ctx_1024t = _ctx_1024t * jax.lax.rsqrt(jnp.mean(jnp.square(_ctx_1024t)) + 1e-12) * 0.953939
        ctx_1024 = 2.81802e-05 + 1.00001 * (_ctx_1024t + 0.3 * jax.random.normal(jax.random.fold_in(_rk, 611), (8, 512, 128), jnp.float32))
        return (x, ctx_1024)
    x, ctx_1024 = _rec_inputs()

    def _L0_attn_setup():
        import jax, jax.numpy as jnp
        import numpy as np
        DIM = 128
        N_HEADS = 16
        HEAD_DIM = DIM // N_HEADS
        D_LATENT = 32
        B, T = (1, 512)
        key = jax.random.key(seed)
        ks = jax.random.split(key, 6)
        s = 0.02
        return {'x': jax.random.normal(ks[0], (B, T, DIM), dtype=jnp.float32), 'W_DKV': jax.random.normal(ks[1], (DIM, D_LATENT), dtype=jnp.float32) * s, 'W_UK': jax.random.normal(ks[2], (D_LATENT, DIM), dtype=jnp.float32) * s, 'W_UV': jax.random.normal(ks[3], (D_LATENT, DIM), dtype=jnp.float32) * s, 'W_UQ': jax.random.normal(ks[4], (DIM, DIM), dtype=jnp.float32) * s, 'W_O': jax.random.normal(ks[5], (DIM, DIM), dtype=jnp.float32) * s}
    _L0_attn_all = _L0_attn_setup()
    _L0_attn_in = {k: v for k, v in _L0_attn_all.items() if k in ('W_DKV', 'W_UK', 'W_UV', 'W_UQ', 'W_O')}
    del _L0_attn_all

    def _L0_xattn_setup():
        import jax, jax.numpy as jnp
        import numpy as np
        D_MODEL = 128
        N_HEADS = 16
        HEAD_DIM = D_MODEL // N_HEADS
        key = jax.random.key(seed)
        k1, k2, k3, k4, k5, k6 = jax.random.split(key, 6)
        B, T_q, T_kv = (4, 128, 512)
        s = 1.0 / np.sqrt(D_MODEL)
        return {'query': jax.random.normal(k1, (B, T_q, D_MODEL), dtype=jnp.float32), 'kv_source': jax.random.normal(k2, (B, T_kv, D_MODEL), dtype=jnp.float32), 'w_q': jax.random.normal(k3, (D_MODEL, D_MODEL), dtype=jnp.float32) * s, 'w_k': jax.random.normal(k4, (D_MODEL, D_MODEL), dtype=jnp.float32) * s, 'w_v': jax.random.normal(k5, (D_MODEL, D_MODEL), dtype=jnp.float32) * s, 'w_o': jax.random.normal(k6, (D_MODEL, D_MODEL), dtype=jnp.float32) * s}
    _L0_xattn_all = _L0_xattn_setup()
    _L0_xattn_in = {k: v for k, v in _L0_xattn_all.items() if k in ('w_q', 'w_k', 'w_v', 'w_o')}
    del _L0_xattn_all

    def _L0_ffn_setup():
        import jax, jax.numpy as jnp
        import numpy as np
        TOP_K = 2
        key = jax.random.key(seed)
        kx, kg, k1, k2 = jax.random.split(key, 4)
        B, T, D, E, H = (4, 128, 128, 8, 256)
        x = jax.random.normal(kx, (B, T, D), dtype=jnp.float32)
        Wg = jax.random.normal(kg, (D, E), dtype=jnp.float32) * 0.02
        W1 = jax.random.normal(k1, (E, D, H), dtype=jnp.float32) * 0.02
        W2 = jax.random.normal(k2, (E, H, D), dtype=jnp.float32) * 0.02
        return {'x': x, 'Wg': Wg, 'W1': W1, 'W2': W2}
    _L0_ffn_all = _L0_ffn_setup()
    _L0_ffn_in = {k: v for k, v in _L0_ffn_all.items() if k in ('Wg', 'W1', 'W2')}
    del _L0_ffn_all
    return {'x': x, 'ctx_1024': ctx_1024, 'L0_attn_W_DKV': _L0_attn_in['W_DKV'], 'L0_attn_W_UK': _L0_attn_in['W_UK'], 'L0_attn_W_UV': _L0_attn_in['W_UV'], 'L0_attn_W_UQ': _L0_attn_in['W_UQ'], 'L0_attn_W_O': _L0_attn_in['W_O'], 'L0_xattn_w_q': _L0_xattn_in['w_q'], 'L0_xattn_w_k': _L0_xattn_in['w_k'], 'L0_xattn_w_v': _L0_xattn_in['w_v'], 'L0_xattn_w_o': _L0_xattn_in['w_o'], 'L0_ffn_Wg': _L0_ffn_in['Wg'], 'L0_ffn_W1': _L0_ffn_in['W1'], 'L0_ffn_W2': _L0_ffn_in['W2']}

def reference(x, ctx_1024, L0_attn_W_DKV, L0_attn_W_UK, L0_attn_W_UV, L0_attn_W_UQ, L0_attn_W_O, L0_xattn_w_q, L0_xattn_w_k, L0_xattn_w_v, L0_xattn_w_o, L0_ffn_Wg, L0_ffn_W1, L0_ffn_W2):
    import jax
    import jax.numpy as jnp

    def _L0_attn_ref(x, W_DKV, W_UK, W_UV, W_UQ, W_O):
        import jax, jax.numpy as jnp
        import numpy as np
        DIM = 128
        N_HEADS = 16
        HEAD_DIM = DIM // N_HEADS
        D_LATENT = 32
        B, T = (1, 512)
        b, t, d = x.shape
        h, hd = (N_HEADS, HEAD_DIM)
        c_kv = x @ W_DKV
        k = (c_kv @ W_UK).reshape(b, t, h, hd)
        v = (c_kv @ W_UV).reshape(b, t, h, hd)
        q = (x @ W_UQ).reshape(b, t, h, hd)
        scale = 1.0 / jnp.sqrt(jnp.asarray(hd, x.dtype))
        scores = jnp.einsum('bqhd,bkhd->bhqk', q, k) * scale
        causal = jnp.tril(jnp.ones((t, t), dtype=bool))
        scores = jnp.where(causal, scores, jnp.asarray(-jnp.inf, scores.dtype))
        probs = jax.nn.softmax(scores, axis=-1)
        ctx = jnp.einsum('bhqk,bkhd->bqhd', probs, v).reshape(b, t, d)
        return ctx @ W_O

    def _L0_xattn_ref(query, kv_source, w_q, w_k, w_v, w_o):
        import jax, jax.numpy as jnp
        import numpy as np
        D_MODEL = 128
        N_HEADS = 16
        HEAD_DIM = D_MODEL // N_HEADS
        B, T_q, _ = query.shape
        T_kv = kv_source.shape[1]
        q = (query @ w_q.T).reshape(B, T_q, N_HEADS, HEAD_DIM)
        k = (kv_source @ w_k.T).reshape(B, T_kv, N_HEADS, HEAD_DIM)
        v = (kv_source @ w_v.T).reshape(B, T_kv, N_HEADS, HEAD_DIM)
        scale = HEAD_DIM ** (-0.5)
        attn = jax.nn.softmax(jnp.einsum('bqhd,bkhd->bhqk', q, k) * scale, axis=-1)
        out = jnp.einsum('bhqk,bkhd->bqhd', attn, v).reshape(B, T_q, D_MODEL)
        return out @ w_o.T

    def _L0_ffn_ref(x, Wg, W1, W2):
        import jax, jax.numpy as jnp
        import numpy as np
        TOP_K = 2
        B, T, D = x.shape
        E = W1.shape[0]
        logits = jnp.einsum('btd,de->bte', x, Wg)
        probs = jax.nn.softmax(logits, axis=-1)
        top_w, top_i = jax.lax.top_k(probs, TOP_K)
        top_w = top_w / (jnp.sum(top_w, axis=-1, keepdims=True) + 1e-08)
        N = B * T
        oh = jax.nn.one_hot(top_i.reshape(N, TOP_K), E, dtype=x.dtype)
        combine = jnp.sum(oh * top_w.reshape(N, TOP_K)[..., None], axis=1)
        xt = x.reshape(N, D)
        h = jnp.einsum('td,edh->teh', xt, W1)
        h = jnp.square(jax.nn.relu(h))
        y = jnp.einsum('teh,ehd->ted', h, W2)
        out = jnp.einsum('te,ted->td', combine, y)
        return out.reshape(B, T, D)
    x = _layernorm(x + _L0_attn_ref(x, L0_attn_W_DKV, L0_attn_W_UK, L0_attn_W_UV, L0_attn_W_UQ, L0_attn_W_O), axis=-1)
    x = _layernorm(x + _L0_xattn_ref(x, ctx_1024, L0_xattn_w_q, L0_xattn_w_k, L0_xattn_w_v, L0_xattn_w_o), axis=-1)
    x = _layernorm(x + _L0_ffn_ref(x, L0_ffn_Wg, L0_ffn_W1, L0_ffn_W2), axis=-1)
    return x

_drawn_inputs = setup_inputs


def setup_inputs(seed=0):
    import zlib

    import numpy as np

    out = dict(_drawn_inputs(seed))
    spreads = {}
    factors = {'L0_attn_W_DKV': 8.0,
     'L0_attn_W_UK': 8.0,
     'L0_attn_W_UV': 8.0,
     'L0_attn_W_UQ': 8.0,
     'L0_attn_W_O': 8.0,
     'L0_ffn_Wg': 4.705,
     'L0_ffn_W1': 4.439,
     'L0_ffn_W2': 4.096}
    for name, (base, spread) in spreads.items():
        noise = np.random.default_rng([zlib.crc32(name.encode()), seed]).standard_normal(out[name].shape)
        drawn = base * np.exp(spread * noise) if base else spread * noise
        out[name] = jnp.asarray(drawn.astype(out[name].dtype))
    for name, factor in factors.items():
        out[name] = (out[name] * factor).astype(out[name].dtype)
    return out
```

```python
from contextlib import ExitStack

import concourse.bass as bass
from concourse import mybir

F32 = mybir.dt.float32
F32R = mybir.dt.float32r
BF16 = mybir.dt.bfloat16
ALU = mybir.AluOpType
ACT = mybir.ActivationFunctionType
AX = mybir.AxisListType

P = 128
B, T, D = 8, 256, 128
TC = 512
H, HD = 16, 8
E, HID = 8, 256
QT = T // P
NT = B * QT
SCALE = float(HD) ** -0.5
LN_EPS = 1e-5
TOPW_EPS = 1e-8
GATE = 17
MASKED = -1e30
KV = 512
VW = 32
ROW_M = 4 * HD


class Phase:

    def __init__(self, causal, keys, batches_per_step, item0, unit0, bank0, step0, batch0):
        self.causal, self.keys = causal, keys
        self.KC = keys // P
        self.bps = batches_per_step
        self.G = 4 * batches_per_step
        self.S = B // batches_per_step
        self.UH = 2 if causal else 1
        self.UN = 4 // self.UH
        self.MB = 4 if causal else 8
        self.item0, self.unit0, self.bank0, self.step0, self.batch0 = item0, unit0, bank0, step0, batch0
        self.qcols = T * batches_per_step
        self.slots = batches_per_step if causal else 4
        self.x0 = 0

    def item(self, i, j):
        return i * self.G + (self.item0 + j)

    def events(self, j, hh, main, nxt, prev):
        G, ev = self.G, []
        if hh == 0 and (main if j + 1 < G else nxt):
            ev.append(("max_T", j + 1))
        if (j, hh) == (0, 1) and nxt:
            ev.append(("K", 0))
        if (j, hh) == (0, 3) and nxt:
            ev.append(("Q", 0))
        if (j, hh) == (2, 1) and nxt:
            ev.append(("V", 0))
        if hh == 2 and (main if j > 0 else prev):
            ev.append(("U_T", j - 1))
        for bb in range(self.bps):
            e = 4 * bb + 3
            for after, slot, name in ((2, 1, "ctx_T"), (2, 3, "out_proj"), (4, 1, "x_T")):
                if (j, hh) == ((e + after) % G, slot) and (main if e + after < G else prev):
                    ev.append((name, bb if e + after < G else bb - self.bps))
        return ev

    def count(self, main, nxt, prev):
        return sum(len(self.events(j, hh, main, nxt, prev)) for j in range(self.G) for hh in range(4))

    def x_start(self, i):
        first = self.count(False, True, False)
        if isinstance(i, int) and i == -1:
            return self.x0
        if isinstance(i, int) and i == 0:
            return self.x0 + first
        second = first + self.count(True, True, False)
        full = self.count(True, True, True)
        if isinstance(i, int) and i == self.S:
            return self.x0 + second + full * (self.S - 2) + self.count(True, False, True)
        return i * full + (self.x0 + second - full)

    def total(self):
        return self.x_start(self.S) + self.count(False, False, True)

    def slots_of_step(self, i, main, nxt, prev):
        x, n = self.x_start(i), 0
        for j in range(self.G):
            for hh in range(4):
                evs = []
                for name, arg in self.events(j, hh, main, nxt, prev):
                    evs.append((name, arg, x + n))
                    n += 1
                yield j, hh, evs


def run_steps(eng, ph, step, last_full=1):
    step(ph, -1, False, True, False)
    step(ph, 0, True, True, False)
    with eng.Fori(1, ph.S - last_full) as i:
        step(ph, i, True, True, True)
    for i in range(ph.S - last_full, ph.S - 1):
        step(ph, i, True, True, True)
    step(ph, ph.S - 1, True, False, True)
    step(ph, ph.S, False, False, True)


def run_blocks(eng, block):
    block(0)
    with eng.Fori(1, 4) as tb:
        block(tb)


def wait(eng, sem, value):
    if not isinstance(value, int) or value > 0:
        eng.wait_ge(sem, value)


def decoder_layer(nc, x_tok_d, kvT_d, wdkvT_d, wuk_d, wuv_d, self_wq_d, self_wo_d,
                  cross_wq_d, cross_wk_d, cross_wv_d, cross_wo_d, wg_d, w1_d, w2_d, out_d):
    SELF = Phase(True, T, 2, 0, 0, 0, 0, 0)
    items, units, banks = B * 4, B * 4 * SELF.UN, B * 4 * SELF.MB
    CROSS = Phase(False, TC, 1, items, units, banks, SELF.S, B)
    SELF.x0 = 1
    CROSS.x0 = SELF.total()
    STEPS = SELF.S + CROSS.S
    XN = CROSS.total()
    ALL_ITEMS, ALL_UNITS, ALL_BANKS = 2 * items, units + B * 4 * CROSS.UN, banks + B * 4 * CROSS.MB

    ctx = ExitStack()
    with ctx:
        def sb(name, shape, dt=F32):
            return ctx.enter_context(nc.sbuf_tensor(name, shape, dt))

        def pb(name, shape):
            return ctx.enter_context(nc.psum_tensor(name, shape, F32))

        def sem(name):
            return ctx.enter_context(nc.semaphore(name))

        x_tok = sb("x_tok", [P, NT, D])
        xT = sb("xT", [P, B * T])
        kvT = sb("kvT", [P, KV])
        w_self = sb("w_self", [P, 4, D])
        w_cross = sb("w_cross", [P, 4, D])
        w_lat = sb("w_lat", [32, 3, D])
        w_gate = sb("w_gate", [P, E])
        w1 = sb("w1", [P, E, HID])
        w2 = sb("w2", [P, E, 2, D])
        ident = sb("ident", [P, P])
        ident_b = sb("ident_b", [P, P], BF16)
        mask_b = sb("mask_b", [P, P], BF16)
        k_parts = sb("k_parts", [P, 2, KV], F32R)
        q_parts = sb("q_parts", [P, 2, KV], F32R)
        k_stack = sb("k_stack", [P, 8192], F32R)
        q_stack = sb("q_stack", [P, 8192], F32R)
        probs = sb("probs", [P, 2, 4096])
        v_new = sb("v_new", [P, KV // P, D])
        v_aug = sb("v_aug", [P, KV // P, H, VW])
        mx = sb("mx", [P, 2, QT, 4])
        mx_row = sb("mx_row", [4, 2, T], F32R)
        u_sb = sb("u_sb", [P, T])
        rden = sb("rden", [P, QT, 4])
        ctxn = sb("ctxn", [P, QT, D])
        ctxT = sb("ctxT", [P, T])
        y_sb = sb("y_sb", [P, 4, D])
        xn = sb("xn", [P, QT, D])
        stats = sb("stats", [P, 4, 6])
        mv = sb("mv", [P, 4, 2])
        rstd = sb("rstd", [P, 4])
        minus_half = sb("minus_half", [P, 4])
        relu = sb("relu", [P, 2, 2, 512])
        act2 = sb("act2", [P, 2, 2, 512])
        lg_sb = sb("lg_sb", [E, 512])
        lmax = sb("lmax", [P, 4])
        lsub = sb("lsub", [P, 4, E])
        lexp = sb("lexp", [P, 4, E])
        lsum = sb("lsum", [P, 4])
        lrec = sb("lrec", [P, 4])
        gp = sb("gp", [P, 4, 2 * E])
        top = sb("top", [P, 4, E])
        rest = sb("rest", [P, 4, 2 * E])
        comb = sb("comb", [P, 4, E])
        acc = sb("acc", [P, 4, D])
        res = sb("res", [P, 4, D])

        ps_s = pb("ps_s", [P, 2, 1024])
        ps_m = pb("ps_m", [P, 2, 512])
        ps_u = pb("ps_u", [P, 512])
        ps_x = pb("ps_x", [P, 512])

        k_scr = [nc.dram_tensor("k_scr_s", (SELF.S, 2, 4, P, T), F32).ap(),
                 nc.dram_tensor("k_scr_c", (CROSS.S, 1, 4, P, TC), F32).ap()]
        q_scr = [nc.dram_tensor("q_scr_s", (SELF.S, 2, 4, P, T), F32).ap(),
                 nc.dram_tensor("q_scr_c", (CROSS.S, 1, 4, P, T), F32).ap()]

        kv_loaded = sem("kv_loaded")
        taken = sem("taken")
        x_loaded = sem("x_loaded")
        lat_loaded = sem("lat_loaded")
        w_loaded = sem("w_loaded")
        ffn_loaded = sem("ffn_loaded")
        init_done = sem("init_done")
        q_stack_zero = sem("q_stack_zero")
        const_done = sem("const_done")
        qk_done = sem("qk_done")
        exp_done = sem("exp_done")
        masked = sem("masked")
        max_done = sem("max_done")
        max_read = sem("max_read")
        q_row_zero = sem("q_row_zero")
        mx_loaded = [sem(f"mx_loaded{p}") for p in range(2)]
        pv_done = sem("pv_done")
        u_read = sem("u_read")
        x_full = sem("x_full")
        x_read = sem("x_read")
        hi_done = sem("hi_done")
        spilled = sem("spilled")
        stack_loaded = [[sem(f"stack{n}_{s}") for s in range(ph.slots)] for n, ph in enumerate((SELF, CROSS))]
        v_spread = sem("v_spread")
        rden_done = sem("rden_done")
        ln_chain = sem("ln_chain")
        mv_ready = sem("mv_ready")
        rstd_chain = sem("rstd_chain")
        x_new = sem("x_new")
        x_kept = sem("x_kept")
        lg_done, lg_read, lt_done, lt_sub, lt_exp = (sem("lg_done"), sem("lg_read"), sem("lt_done"),
                                                     sem("lt_sub"), sem("lt_exp"))
        gate_chain = sem("gate_chain")
        h_done, relu_done, sq_done = sem("h_done"), sem("relu_done"), sem("sq_done")
        y_done, acc_chain = sem("y_done"), sem("acc_chain")
        fin_chain, fin_mv, fin_rstd = sem("fin_chain"), sem("fin_mv"), sem("fin_rstd")
        fin_done = sem("fin_done")
        stored = sem("stored")

        def apart(eng):
            eng.sem_inc(taken, 1)

        PH = {SELF: 0, CROSS: 1}
        W = {SELF: w_self, CROSS: w_cross}

        def xcol(ph, i):
            return i * ph.qcols

        def unit_before(ph, w):
            return (w - ph.item0) * ph.UN + ph.unit0

        def k_view(ph, slot_item, hh):
            n = (4 * slot_item + hh) * ph.keys
            return k_stack[:, n:n + ph.keys]

        def q_view(ph, slot_item, hh, q0=0, q1=T):
            n = (4 * slot_item + hh) * T
            return q_stack[:, n + q0:n + q1]

        block = ctx.enter_context(nc.Block())

        @block.sync
        def _(sp):
            sp.dma_start(w_lat[:, 0, :], wdkvT_d).then_inc(lat_loaded, 16)
            sp.dma_start(w_lat[:, 1, :], wuk_d).then_inc(lat_loaded, 16)
            sp.dma_start(w_lat[:, 2, :], wuv_d).then_inc(lat_loaded, 16)
            sp.dma_start(kvT[:, :], kvT_d[0]).then_inc(kv_loaded, 16)

            def step(ph, i, main, nxt, prev, load=True):
                n = PH[ph]
                for j, hh, evs in ph.slots_of_step(i, main, nxt, prev):
                    for name, arg, x in evs:
                        if name == "max_T":
                            w = ph.item(i, arg)
                            par = (ph.item0 + arg) % 2
                            half = i * (ph.G // 2) + (ph.item0 + arg) // 2
                            sp.wait_ge(x_read, x + 1)
                            c = (arg % ph.G) * 4 * T
                            sp.dma_start(q_stack[ROW_M:ROW_M + 1, c:c + 4 * T].bitcast(F32),
                                         mx_row[:, par, :].bitcast(F32)).then_inc(mx_loaded[par], 16)
                        if name in ("K", "Q"):
                            sp.wait_ge(x_read, x + 1)
                            apart(sp)
                            parts = k_parts if name == "K" else q_parts
                            width = ph.keys if name == "K" else T
                            for bb in range(ph.bps):
                                scr = (k_scr if name == "K" else q_scr)[n][i + 1, bb]
                                order = "(rep hl) p k -> rep p hl k" if name == "K" else "(hl rep) p k -> rep p hl k"
                                dst = scr.rearrange(order, rep=2)
                                for rep in range(2):
                                    sp.dma_start(dst[rep], parts[:, :, bb * width:(bb + 1) * width].bitcast(F32))\
                                      .then_inc(spilled, 16)
                        if name == "V" and load:
                            sp.wait_ge(x_full, x + 1)
                            apart(sp)
                            sp.dma_start(kvT[:, :], kvT_d[i + (ph.step0 + 2)]).then_inc(kv_loaded, 16)
                    per = ph.G // ph.slots
                    if hh == 3 and nxt and j % per == per - 1:
                        slot = j // per
                        w = ph.item(i, j)
                        if main:
                            sp.wait_ge(qk_done, unit_before(ph, w + 1))
                            apart(sp)
                        elif ph is CROSS:
                            sp.wait_ge(qk_done, units)
                        else:
                            sp.wait_ge(const_done, 1)
                            sp.wait_ge(q_stack_zero, 1)
                        before = 0 if ph is SELF else 16 * 8 * SELF.S
                        sp.wait_ge(spilled, (i + 2) * (16 * 4 * ph.bps) + before)
                        apart(sp)
                        for scr, stack, width in ((k_scr[n], k_stack, ph.keys), (q_scr[n], q_stack, T)):
                            cols = per * 4 * width
                            if ph is SELF:
                                src = scr[i + 1, slot].rearrange("r (d h) k -> r d (h k)", d=HD)
                            else:
                                src = scr[i + 1, 0, :, 32 * slot:32 * slot + 32, :]\
                                    .rearrange("r (d h) k -> r d (h k)", d=HD)
                            sp.dma_start(stack[0:4 * HD, slot * cols:(slot + 1) * cols].bitcast(F32), src)\
                              .then_inc(stack_loaded[n][slot], 16)

            step(SELF, -1, False, True, False)
            step(SELF, 0, True, True, False)
            with sp.Fori(1, SELF.S - 1) as i:
                step(SELF, i, True, True, True)
            step(SELF, SELF.S - 1, True, False, True)
            step(CROSS, -1, False, True, False)
            step(CROSS, 0, True, True, False)
            with sp.Fori(1, CROSS.S - 2) as i:
                step(CROSS, i, True, True, True)
            step(CROSS, CROSS.S - 2, True, True, True, load=False)
            step(CROSS, CROSS.S - 1, True, False, True)
            out_v = out_d.rearrange("(b t p) d -> b p t d", t=4, p=P)
            with sp.Fori(0, 4) as tb:
                sp.wait_ge(fin_done, tb * 4 + 4)
                apart(sp)
                sp.dma_start(out_v[tb], res[:, :, :]).then_inc(stored, 16)
            sp.wait_ge(stored, 16 * 4)

        @block.gpsimd
        def _(pool):
            pool.memset(ident[:, :], 0.0).then_inc(init_done, 1)
            pool.memset(ident_b[:, :], 0.0).then_inc(init_done, 1)
            pool.memset(mask_b[:, :], 0.0).then_inc(init_done, 1)
            pool.memset(k_stack[:, :].bitcast(F32), 0.0).then_inc(init_done, 1)
            pool.memset(v_aug[:, :, :, :].rearrange("p a b c -> p (a b c)"), 0.0).then_inc(init_done, 1)
            pool.wait_ge(init_done, 5)
            for m in (ident, ident_b):
                pool.affine_select(out=m[:, :], in_=m[:, :], compare_op=ALU.not_equal, fill=1.0, base=0,
                                   pattern=[[-1, P]], channel_multiplier=1).then_inc(init_done, 1)
            pool.affine_select(out=mask_b[:, :], in_=mask_b[:, :], compare_op=ALU.is_ge, fill=MASKED, base=0,
                               pattern=[[-1, P]], channel_multiplier=1).then_inc(init_done, 1)
            pool.memset(v_aug[:, :, :, HD:HD + 1].rearrange("p a b c -> p (a b c)"), 1.0).then_inc(init_done, 1)
            pool.memset(gp[:, :, E:2 * E], -1.0).then_inc(init_done, 1)
            pool.memset(minus_half[:, :], -0.5).then_inc(init_done, 1)
            pool.wait_ge(init_done, 11)
            pool.memset(k_stack[ROW_M:ROW_M + 1, :].bitcast(F32), -1.0).then_inc(init_done, 1)
            pool.wait_ge(init_done, 12)
            pool.memset(top[:, :, :], -1.0).then_inc(const_done, 1)

            def normalise(y, out, tiles, chain, base, done):
                apart(pool)
                pool.tensor_scalar(rstd[:, 0:tiles], mv[:, 0:tiles, 1], LN_EPS, 1.0, ALU.add, ALU.mult)\
                    .then_inc(chain, 1)
                pool.wait_ge(chain, base + 1)
                pool.tensor_tensor(rstd[:, 0:tiles], rstd[:, 0:tiles], minus_half[:, 0:tiles], ALU.pow)\
                    .then_inc(chain, 1)
                pool.wait_ge(chain, base + 2)
                apart(pool)
                for t in range(tiles):
                    pool.tensor_scalar(out[:, t, :], y[:, t, :], mv[:, t, 0:1], rstd[:, t:t + 1],
                                       ALU.subtract, ALU.mult).then_inc(done, 1)

            def step(ph, i, main, nxt, prev):
                for j in range(ph.G):
                    w = ph.item(i, j)
                    if j == 0 and main:
                        pool.wait_ge(x_read, ph.x_start(i))
                        wait(pool, pv_done, w)
                        apart(pool)
                        pool.tensor_scalar(v_aug[:, :, :, 0:HD],
                                           v_new[:, :, :].rearrange("p c (h d) -> p c h d", d=HD),
                                           1.0, 0.0, ALU.mult, ALU.add).then_inc(v_spread, 1)
                        pool.wait_ge(v_spread, i + (ph.step0 + 1))
                    if main and ph.causal:
                        pool.wait_ge(exp_done, unit_before(ph, w + 1))
                        apart(pool)
                        pr = probs[:, j % 2, 0:2048].rearrange("p (b q) -> p b q", q=256)[:, :, 0:P]
                        pool.affine_select(out=pr, in_=pr, compare_op=ALU.is_ge, fill=0.0, base=0,
                                           pattern=[[0, 8], [1, P]], channel_multiplier=-1)\
                            .then_inc(masked, 1)
                    if main:
                        pool.wait_ge(qk_done, unit_before(ph, w + 1))
                        apart(pool)
                        if ph.causal:
                            pool.wait_ge(masked, w + 1)
                            apart(pool)
                        c = j * 4 * T
                        pool.memset(q_stack[ROW_M:ROW_M + 1, c:c + 4 * T].bitcast(F32), 0.0).then_inc(q_row_zero, 1)
                        pool.wait_ge(q_row_zero, w + 1)
                    for bb in range(ph.bps):
                        e = 4 * bb + 3
                        if j == (e + 3) % ph.G and (main if e + 3 < ph.G else prev):
                            b = i * ph.bps + (bb if e + 3 < ph.G else bb - ph.bps)
                            bn = b + ph.batch0
                            pool.wait_ge(mv_ready, bn + 1)
                            normalise(y_sb, xn, QT, rstd_chain, bn * 2, x_new)
                            pool.wait_ge(x_new, bn * QT + QT)
                            apart(pool)
                            pool.tensor_copy(x_tok[:, bass.ds(b * QT, QT), :], xn[:, :, :]).then_inc(x_kept, 1)
                            pool.wait_ge(x_kept, bn + 1)

            for ph in (SELF, CROSS):
                run_steps(pool, ph, step)

            def block_(tb):
                for e in range(E):
                    n = tb * (2 * E) + 2 * e
                    for c in range(2):
                        pool.wait_ge(relu_done, n + (c + 1))
                        wait(pool, y_done, tb * E + (e - 1))
                        pool.tensor_tensor(act2[:, e % 2, c, :], relu[:, e % 2, c, :], relu[:, e % 2, c, :],
                                           ALU.mult).then_inc(sq_done, 1)
                pool.wait_ge(fin_mv, tb * 4 + 4)
                wait(pool, stored, tb * 16)
                normalise(acc, res, 4, fin_rstd, tb * 2, fin_done)

            run_blocks(pool, block_)

        @block.scalar
        def _(act):
            def copy(out, in_):
                return nc.scalar.activation(out, in_, ACT.Copy)

            act.dma_start(w_self[:, 0, :], self_wq_d).then_inc(w_loaded, 16)
            act.dma_start(w_self[:, 3, :], self_wo_d).then_inc(w_loaded, 16)
            act.dma_start(x_tok[:, :, :], x_tok_d.rearrange("(t p) d -> p t d", p=P)).then_inc(x_loaded, 16)
            for n, d in enumerate((cross_wq_d, cross_wk_d, cross_wv_d, cross_wo_d)):
                act.dma_start(w_cross[:, n, :], d).then_inc(w_loaded, 16)
            act.dma_start(w_gate[:, :], wg_d).then_inc(ffn_loaded, 16)
            act.dma_start(w1[:, :, :], w1_d).then_inc(ffn_loaded, 16)
            act.dma_start(w2[:, :, :, :], w2_d).then_inc(ffn_loaded, 16)
            act.wait_ge(x_full, 1)
            copy(w_self[:, 1:3, :].rearrange("p a b -> p (a b)"), ps_x[:, 0:2 * D]).then_inc(x_read, 1)

            def step(ph, i, main, nxt, prev):
                for j, hh, evs in ph.slots_of_step(i, main, nxt, prev):
                    w = ph.item(i, j)
                    if main and hh % ph.UH == 0:
                        u = hh // ph.UH
                        n = unit_before(ph, w) + u
                        act.wait_ge(qk_done, n + 1)
                        if hh == 0:
                            wait(act, pv_done, w - 1)
                        if ph.causal:
                            nc.scalar.activation(
                                probs[:, j % 2, u * 1024:u * 1024 + 1024]
                                .rearrange("p (h c) -> p h c", h=2)[:, :, 0:384],
                                ps_s[:, u % 2, :].rearrange("p (h c) -> p h c", h=2)[:, :, 0:384],
                                ACT.Exp, scale=SCALE).then_inc(exp_done, 1)
                        else:
                            nc.scalar.activation(probs[:, j % 2, hh * 1024:hh * 1024 + 1024], ps_s[:, u % 2, :],
                                                 ACT.Exp, scale=SCALE).then_inc(exp_done, 1)
                    if hh == 0 and (main if j > 0 else prev):
                        act.wait_ge(pv_done, w)
                        copy(u_sb[:, :], ps_u[:, 0:T]).then_inc(u_read, 1)
                    for name, arg, x in evs:
                        if name == "max_T":
                            act.wait_ge(x_full, x + 1)
                            par = (ph.item0 + arg) % 2
                            copy(mx_row[:, par, :], ps_x[0:4, 0:T]).then_inc(x_read, 1)
                        if name == "K":
                            act.wait_ge(x_full, x + 1)
                            copy(k_parts[:, 0, :], ps_x[:, 0:KV]).then_inc(hi_done, 1)
                        if name == "Q":
                            act.wait_ge(x_full, x + 1)
                            copy(q_parts[:, 0, 0:ph.qcols], ps_x[:, 0:ph.qcols]).then_inc(hi_done, 1)
                        if name == "V":
                            act.wait_ge(x_full, x + 1)
                            if not (isinstance(i, int) and i < 0 and ph is SELF):
                                act.wait_ge(v_spread, i + (ph.step0 + 1))
                            copy(v_new[:, :, :].rearrange("p c n -> p (c n)"), ps_x[:, 0:KV]).then_inc(x_read, 1)
                        if name == "ctx_T":
                            act.wait_ge(x_full, x + 1)
                            copy(ctxT[:, :], ps_x[:, 0:T]).then_inc(x_read, 1)
                        if name == "x_T":
                            act.wait_ge(x_full, x + 1)
                            b = i * ph.bps + arg
                            copy(xT[:, bass.ds(b * T, T)], ps_x[:, 0:T]).then_inc(x_read, 1)

            for ph in (SELF, CROSS):
                run_steps(act, ph, step)

            def block_(tb):
                act.wait_ge(lg_done, tb + 1)
                wait(act, lt_done, tb)
                copy(lg_sb[:, :], ps_x[0:E, 0:512]).then_inc(lg_read, 1)
                for e in range(E):
                    if e == 1:
                        act.wait_ge(lt_sub, tb + 1)
                        nc.scalar.activation(lexp[:, :, :], lsub[:, :, :], ACT.Exp).then_inc(lt_exp, 1)
                    for c in range(2):
                        n = tb * (2 * E) + (2 * e + c)
                        act.wait_ge(h_done, n + 1)
                        wait(act, sq_done, n - 3)
                        nc.scalar.activation(relu[:, e % 2, c, :], ps_s[:, e % 2, 512 * c:512 * c + 512],
                                             ACT.Relu).then_inc(relu_done, 1)

            run_blocks(act, block_)

        @block.vector
        def _(dve):
            v = nc.vector
            v.memset(q_stack[:, :].bitcast(F32), 0.0).then_inc(q_stack_zero, 1)
            dve.wait_ge(x_loaded, 16)

            def moments(y, tiles, chain, base, done):
                for t in range(tiles):
                    v.bn_stats(stats[:, t, :], y[:, t, :]).then_inc(chain, 1)
                dve.wait_ge(chain, base + tiles)
                apart(dve)
                for t in range(tiles):
                    done(t, v.bn_aggr(mv[:, t, :], stats[:, t, :]))

            def step(ph, i, main, nxt, prev):
                for j, hh, evs in ph.slots_of_step(i, main, nxt, prev):
                    w = ph.item(i, j)
                    if main if j + 2 < ph.G else nxt:
                        par = j % 2
                        if ph.causal:
                            n = (w + 2 - ph.item0) * 4 + (ph.bank0 + hh)
                            dve.wait_ge(max_done, n + 1)
                            v.tensor_reduce(out=mx[:, par, 0, hh:hh + 1], in_=ps_m[:, hh % 2, 0:P],
                                            axis=AX.X, op=ALU.max)
                            v.tensor_reduce(out=mx[:, par, 1, hh:hh + 1], in_=ps_m[:, hh % 2, P:3 * P],
                                            axis=AX.X, op=ALU.max).then_inc(max_read, 1)
                        else:
                            for t in range(QT):
                                n = (w + 2 - ph.item0) * 8 + (ph.bank0 + 2 * hh + t)
                                dve.wait_ge(max_done, n + 1)
                                v.tensor_reduce(out=mx[:, par, t, hh:hh + 1], in_=ps_m[:, t, :],
                                                axis=AX.X, op=ALU.max).then_inc(max_read, 1)
                    for name, arg, x in evs:
                        if name in ("K", "Q"):
                            n = (i + 1) * 2 + (2 * ph.step0 + (name == "Q"))
                            dve.wait_ge(hi_done, n + 1)
                            parts, cols = (k_parts, KV) if name == "K" else (q_parts, ph.qcols)
                            v.tensor_tensor(parts[:, 1, 0:cols], ps_x[:, 0:cols],
                                            parts[:, 0, 0:cols].bitcast(F32), ALU.subtract).then_inc(x_read, 1)
                        if name == "U_T":
                            dve.wait_ge(x_full, x + 1)
                            it = i * ph.G + (ph.item0 + arg)
                            g = arg % 4
                            u = ps_x[:, 0:T].rearrange("p (t h c) -> p t h c", t=QT, c=VW)
                            v.reciprocal(rden[:, :, :], u[:, :, :, HD]).then_inc(rden_done, 1)
                            dve.wait_ge(rden_done, it + 1)
                            o = ctxn[:, :, 32 * g:32 * g + 32].rearrange("p t (h c) -> p t h c", c=HD)
                            v.tensor_tensor(o, u[:, :, :, 0:HD],
                                            rden[:, :, :, None].broadcast_to([P, QT, 4, HD]),
                                            ALU.mult).then_inc(x_read, 1)
                        if name == "out_proj":
                            dve.wait_ge(x_full, x + 1)
                            b = i * ph.bps + arg
                            bn = b + ph.batch0
                            if ph is CROSS:
                                dve.wait_ge(x_kept, B)
                            wait(dve, x_new, bn * QT)
                            v.tensor_tensor(y_sb[:, 0:QT, :],
                                            ps_x[:, 0:T].rearrange("p (t d) -> p t d", t=QT),
                                            x_tok[:, bass.ds(b * QT, QT), :], ALU.add).then_inc(x_read, 1)
                            dve.wait_ge(x_read, x + 1)

                            def done(t, ins):
                                if t == QT - 1:
                                    ins.then_inc(mv_ready, 1)
                            moments(y_sb, QT, ln_chain, bn * QT, done)

            for ph in (SELF, CROSS):
                run_steps(dve, ph, step)

            def block_(tb):
                g0 = tb * GATE

                def link(ins, n):
                    ins.then_inc(gate_chain, 1)
                    dve.wait_ge(gate_chain, g0 + n)
                    apart(dve)

                def acc_expert(e):
                    dve.wait_ge(y_done, tb * E + (e + 1))
                    for t in range(4):
                        src = x_tok[:, bass.ds(tb * 4 + t, 1), :].rearrange("p a d -> p (a d)") if e == 0 \
                            else acc[:, t, :]
                        v.scalar_tensor_tensor(acc[:, t, :], ps_m[:, e % 2, t * D:(t + 1) * D],
                                               comb[:, t, e:e + 1], src, op0=ALU.mult, op1=ALU.add)\
                            .then_inc(acc_chain, 1)

                dve.wait_ge(lt_done, tb + 1)
                lt = ps_u[:, 0:4 * E].rearrange("p (t e) -> p t e", t=4)
                link(v.tensor_reduce(out=lmax[:, :], in_=lt, axis=AX.X, op=ALU.max), 1)
                v.tensor_tensor(lsub[:, :, :], lt, lmax[:, :, None].broadcast_to([P, 4, E]),
                                ALU.subtract).then_inc(lt_sub, 1)
                dve.wait_ge(lt_exp, tb + 1)
                link(v.tensor_reduce(out=lsum[:, :], in_=lexp[:, :, :], axis=AX.X, op=ALU.add), 2)
                link(v.reciprocal(lrec[:, :], lsum[:, :]), 3)
                link(v.tensor_tensor(gp[:, :, 0:E], lexp[:, :, :], lrec[:, :, None].broadcast_to([P, 4, E]),
                                     ALU.mult), 4)
                for t in range(4):
                    v.max(out=rest[:, t, 0:E], in_=gp[:, t, 0:E]).then_inc(gate_chain, 1)
                dve.wait_ge(gate_chain, g0 + 8)
                link(v.tensor_copy(top[:, :, 0:2], rest[:, :, 0:2]), 9)
                link(v.scalar_tensor_tensor(lsum[:, :], top[:, :, 0], TOPW_EPS, top[:, :, 1],
                                            op0=ALU.add, op1=ALU.add), 10)
                link(v.reciprocal(lrec[:, :], lsum[:, :]), 11)
                for t in range(4):
                    v.match_replace(out=rest[:, t, :], in_to_replace=top[:, t, :], in_values=gp[:, t, :],
                                    imm_value=0.0).then_inc(gate_chain, 1)
                dve.wait_ge(gate_chain, g0 + 15)
                link(v.tensor_tensor(comb[:, :, :], gp[:, :, 0:E], rest[:, :, 0:E], ALU.subtract), 16)
                link(v.tensor_tensor(comb[:, :, :], comb[:, :, :], lrec[:, :, None].broadcast_to([P, 4, E]),
                                     ALU.mult), 17)
                for e in range(E):
                    if e > 0:
                        dve.wait_ge(acc_chain, tb * (4 * E) + 4 * e)
                    else:
                        wait(dve, fin_done, tb * 4)
                    acc_expert(e)
                dve.wait_ge(acc_chain, tb * (4 * E) + 4 * E)

                def done(t, ins):
                    ins.then_inc(fin_mv, 1)
                moments(acc, 4, fin_chain, tb * 4, done)

            run_blocks(dve, block_)

        @block.tensor
        def _(pe):
            mm = nc.tensor.matmul
            pe.wait_ge(lat_loaded, 48)
            for n in range(2):
                last = mm(ps_x[:, n * D:(n + 1) * D], w_lat[:, 0, :], w_lat[:, 1 + n, :], start=True, stop=True)
            last.then_inc(x_full, 1)
            pe.wait_ge(const_done, 1)

            def step(ph, i, main, nxt, prev):
                n_ph = PH[ph]
                for j, hh, evs in ph.slots_of_step(i, main, nxt, prev):
                    w = ph.item(i, j)
                    if main and hh % ph.UH == 0:
                        u = hh // ph.UH
                        if hh == 0:
                            par = (ph.item0 + j) % 2
                            pe.wait_ge(mx_loaded[par], i * (8 * ph.G) + 16 * ((ph.item0 + j) // 2 + 1))
                        wait(pe, exp_done, unit_before(ph, w) + (u - 1))
                        for h in range(hh, hh + ph.UH):
                            for c in range(ph.KC):
                                q0 = c * P if ph.causal else 0
                                col = (h - hh) * 512 + c * T
                                last = mm(ps_s[:, u % 2, col:col + T - q0],
                                          k_view(ph, j, h)[:, c * P:(c + 1) * P], q_view(ph, j, h, q0, T),
                                          start=True, stop=True)
                        last.then_inc(qk_done, 1)
                    if main if j + 2 < ph.G else nxt:
                        jj = (j + 2) % ph.G
                        if hh == 0:
                            slot = jj // (ph.G // ph.slots)
                            k = i if j + 2 < ph.G else i + 1
                            pe.wait_ge(stack_loaded[n_ph][slot], k * 32 + 32)
                            if ph is CROSS and isinstance(k, int) and k == 0:
                                pe.wait_ge(q_row_zero, items)
                            else:
                                wait(pe, q_row_zero, w + 2 - ph.G + 1)
                        if ph.causal:
                            n = (w + 2) * 4 + hh
                            wait(pe, max_read, n - 1)
                            m = ps_m[:, hh % 2, 0:512].rearrange("p (b q) -> p b q", q=256)[:, :, 0:P]
                            kv = k_view(ph, jj, hh)
                            mm(ps_m[:, hh % 2, 0:P], q_view(ph, jj, hh, 0, P), kv[:, 0:P], start=True, stop=False)
                            mm(ps_m[:, hh % 2, P:3 * P], q_view(ph, jj, hh, P, T), kv, start=False, stop=False)
                            mm(m, ident_b[:, :], mask_b[:, None, :].broadcast_to([P, 2, P]),
                               start=False, stop=True).then_inc(max_done, 1)
                        else:
                            for t in range(QT):
                                n = (w + 2 - ph.item0) * 8 + (ph.bank0 + 2 * hh + t)
                                wait(pe, max_read, n - 1)
                                mm(ps_m[:, t, :], q_view(ph, jj, hh, t * P, (t + 1) * P), k_view(ph, jj, hh),
                                   start=True, stop=True).then_inc(max_done, 1)
                    if hh == 0 and (main if j > 0 else prev):
                        if ph.causal:
                            pe.wait_ge(masked, w)
                        else:
                            pe.wait_ge(exp_done, unit_before(ph, w))
                        pe.wait_ge(v_spread, i + (ph.step0 + (1 if j > 0 else 0)))
                        wait(pe, u_read, w - 1)
                        jp = (j - 1) % ph.G
                        g, c0 = jp % 4, (jp // 4) * ph.KC
                        for c in range(ph.KC):
                            for h in range(4):
                                q0 = c * P if ph.causal else 0
                                col = h * (512 if ph.causal else 1024) + c * T
                                last = mm(ps_u[32 * h:32 * h + 32, q0:T], v_aug[:, c0 + c, 4 * g + h, :],
                                          probs[:, jp % 2, col:col + T - q0],
                                          start=(c == 0), stop=(c == ph.KC - 1))
                        last.then_inc(pv_done, 1)
                    for name, arg, x in evs:
                        wait(pe, x_read, x)
                        if name == "max_T":
                            it = i * ph.G + arg
                            pe.wait_ge(max_read, it * ph.MB + (ph.bank0 + ph.MB))
                            for t in range(QT):
                                last = nc.tensor.transpose(ps_x[0:4, t * P:(t + 1) * P], mx[:, arg % 2, t, :],
                                                           ident[:, :])
                        if name == "K":
                            pe.wait_ge(kv_loaded, i * 16 + 16 * (ph.step0 + 2))
                            if ph is CROSS and isinstance(i, int) and i < 0:
                                pe.wait_ge(w_loaded, 16 * 6)
                            last = mm(ps_x[:, 0:KV], W[ph][:, 1, :], kvT[:, :], start=True, stop=True)
                        if name == "Q":
                            if ph is SELF:
                                if isinstance(i, int) and i < 0:
                                    pe.wait_ge(w_loaded, 16 * 6)
                                src = kvT[:, :]
                            elif isinstance(i, int):
                                src = xT[:, (i + 1) * T:(i + 2) * T]
                            else:
                                src = xT[:, bass.ds((i + 1) * T, T)]
                            last = mm(ps_x[:, 0:ph.qcols], W[ph][:, 0, :], src, start=True, stop=True)
                        if name == "V":
                            for c in range(KV // P):
                                last = mm(ps_x[:, c * D:(c + 1) * D], kvT[:, c * P:(c + 1) * P], W[ph][:, 2, :],
                                          start=True, stop=True)
                        if name == "U_T":
                            pe.wait_ge(u_read, w)
                            for t in range(QT):
                                last = nc.tensor.transpose(ps_x[:, t * P:(t + 1) * P], u_sb[:, t * P:(t + 1) * P],
                                                           ident[:, :])
                        if name == "ctx_T":
                            for t in range(QT):
                                last = nc.tensor.transpose(ps_x[:, t * P:(t + 1) * P], ctxn[:, t, :], ident[:, :])
                        if name == "out_proj":
                            for t in range(QT):
                                last = mm(ps_x[:, t * D:(t + 1) * D], ctxT[:, t * P:(t + 1) * P], W[ph][:, 3, :],
                                          start=True, stop=True)
                        if name == "x_T":
                            pe.wait_ge(x_new, i * (QT * ph.bps) + QT * (ph.batch0 + arg + 1))
                            for t in range(QT):
                                last = nc.tensor.transpose(ps_x[:, t * P:(t + 1) * P], xn[:, t, :], ident[:, :])
                        last.then_inc(x_full, 1)

            for ph in (SELF, CROSS):
                run_steps(pe, ph, step)

            pe.wait_ge(ffn_loaded, 48)
            pe.wait_ge(x_read, XN)
            pe.wait_ge(exp_done, ALL_UNITS)
            pe.wait_ge(max_read, ALL_BANKS)
            pe.wait_ge(x_kept, 2 * B)

            def block_(tb):
                toks = xT[:, bass.ds(tb * 512, 512)]

                def second(e):
                    wait(pe, acc_chain, tb * (4 * E) + 4 * (e - 1))
                    pe.wait_ge(sq_done, tb * (2 * E) + (2 * e + 2))
                    for t in range(4):
                        for c in range(2):
                            last = mm(ps_m[:, e % 2, t * D:(t + 1) * D], act2[:, e % 2, c, t * P:(t + 1) * P],
                                      w2[:, e, c, :], start=(c == 0), stop=(c == 1))
                    last.then_inc(y_done, 1)

                wait(pe, lg_read, tb)
                mm(ps_x[0:E, 0:512], w_gate[:, :], toks, start=True, stop=True).then_inc(lg_done, 1)
                for e in range(E):
                    for c in range(2):
                        wait(pe, relu_done, tb * (2 * E) + (2 * e + c - 3))
                        mm(ps_s[:, e % 2, 512 * c:512 * c + 512], w1[:, e, c * P:(c + 1) * P], toks,
                           start=True, stop=True).then_inc(h_done, 1)
                    if e == 0:
                        pe.wait_ge(lg_read, tb + 1)
                        wait(pe, lt_sub, tb)
                        apart(pe)
                        for t in range(4):
                            last = nc.tensor.transpose(ps_u[:, t * E:(t + 1) * E], lg_sb[:, t * P:(t + 1) * P],
                                                       ident[0:E, 0:E])
                        last.then_inc(lt_done, 1)
                    if e > 0:
                        second(e - 1)
                second(E - 1)

            run_blocks(pe, block_)


def kernel(x, ctx_1024, L0_attn_W_DKV, L0_attn_W_UK, L0_attn_W_UV, L0_attn_W_UQ, L0_attn_W_O,
           L0_xattn_w_q, L0_xattn_w_k, L0_xattn_w_v, L0_xattn_w_o, L0_ffn_Wg, L0_ffn_W1, L0_ffn_W2):
    import numpy as np
    import concourse.bacc as bacc
    from concourse.bass_utils import run_bass_kernel_spmd

    a = {n: np.asarray(v) for n, v in locals().items() if n[0] in "xcL"}
    x, ctx_kv = a["x"], a["ctx_1024"]
    by_dim = np.arange(D).reshape(H, HD).T.reshape(-1)
    by_group = np.arange(D).reshape(4, 4, HD).transpose(0, 2, 1).reshape(-1)
    kvT = np.concatenate([x.reshape(B // 2, KV, D).transpose(0, 2, 1), ctx_kv.transpose(0, 2, 1)])
    arrays = {
        "x_tok": x.reshape(B * T, D),
        "kvT": kvT,
        "wdkvT": a["L0_attn_W_DKV"].T,
        "wuk": a["L0_attn_W_UK"][:, by_dim],
        "wuv": a["L0_attn_W_UV"],
        "self_wq": a["L0_attn_W_UQ"][:, by_dim],
        "self_wo": a["L0_attn_W_O"],
        "cross_wq": a["L0_xattn_w_q"].T[:, by_group],
        "cross_wk": a["L0_xattn_w_k"].T[:, by_group],
        "cross_wv": a["L0_xattn_w_v"].T,
        "cross_wo": a["L0_xattn_w_o"].T,
        "wg": a["L0_ffn_Wg"],
        "w1": a["L0_ffn_W1"].transpose(1, 0, 2),
        "w2": a["L0_ffn_W2"].reshape(E, 2, P, D).transpose(2, 0, 1, 3),
    }
    arrays = {f"{n}_dram": np.ascontiguousarray(v) for n, v in arrays.items()}
    nc = bacc.Bacc("TRN2", target_bir_lowering=False, num_devices=1)
    args = [nc.dram_tensor(n, v.shape, mybir.dt.from_np(v.dtype), kind="ExternalInput").ap()
            for n, v in arrays.items()]
    out = nc.dram_tensor("out_dram", (B * T, D), F32, kind="ExternalOutput").ap()
    decoder_layer(nc, *args, out)
    r = run_bass_kernel_spmd(nc, [arrays], core_ids=[0])
    return r.results[0]["out_dram"].reshape(B, T, D)
```

```python
from contextlib import ExitStack

import concourse.bass as bass
from concourse import mybir

F32 = mybir.dt.float32
F32R = mybir.dt.float32r
BF16 = mybir.dt.bfloat16
ALU = mybir.AluOpType
ACT = mybir.ActivationFunctionType
AX = mybir.AxisListType

P = 128
B, T, D = 8, 256, 128
TC = 512
H, HD = 16, 8
E, HID = 8, 256
QT = T // P
NT = B * QT
SCALE = float(HD) ** -0.5
LN_EPS = 1e-5
TOPW_EPS = 1e-8
GATE = 17
MASKED = -1e30
KV = 512
VW = 32
ROW_M = 4 * HD


class Phase:

    def __init__(self, n, causal, keys, batches_per_step, ahead, item0, unit0, bank0, step0, batch0):
        self.n, self.causal, self.keys = n, causal, keys
        self.KC = keys // P
        self.bps = batches_per_step
        self.ahead = ahead
        self.G = 4 * batches_per_step
        self.S = B // batches_per_step
        self.UH = 2 if causal else 1
        self.UN = 4 // self.UH
        self.MB = 4 if causal else 8
        self.item0, self.unit0, self.bank0, self.step0, self.batch0 = item0, unit0, bank0, step0, batch0
        self.qcols = T * batches_per_step
        self.slots = 4
        self.at = {"K": (0, 2), "Q": (1, 0), "V": (4, 3)} if causal else {"V": (1, 2), "K": (3, 0), "Q": (3, 2)}
        self.lead = {"K": 1, "Q": 1, "V": 1} if causal else {"V": 1, "K": 2, "Q": 2}
        self.load_at = [(2, 3), (3, 3), (5, 3), (7, 3)] if causal else [(0, 3), (1, 3), (2, 3), (3, 3)]
        self.pv_chunks = [(), (), (0,), (1,)] if causal else [(), (0,), (1,), (2, 3)]
        self.x_before = {}

    def item(self, i, j):
        return i * self.G + (self.item0 + j)

    def units(self, i, j):
        return i * (self.G * self.UN) + (self.unit0 + j * self.UN)

    def banks(self, i, j):
        return i * (self.G * self.MB) + (self.bank0 + j * self.MB)

    def later(self, i, j, less, main, nxt):
        t = j + self.ahead - less
        if t < self.G:
            return (self, i, t) if main else None
        if nxt is self:
            return self, i, t
        if nxt is not None and j + nxt.ahead - less >= self.G:
            return nxt, 0, j + nxt.ahead - less - self.G
        return None

    def earlier(self, i, j, back, main, prev):
        if j >= back:
            return (self, i, j - back) if main else None
        if prev is self:
            return self, i, j - back
        return (prev, prev.S - 1, j - back + prev.G) if prev else None

    def events(self, i, j, hh, main, nxt, prev):
        ev = []
        if hh == 1:
            t = self.later(i, j, 1, main, nxt)
            if t:
                ev.append(("max_T",) + t)
        if nxt is self:
            for name, lead in self.lead.items():
                if (j, hh) == self.at[name] and not (isinstance(i, int) and i + lead >= self.S):
                    ev.append((name, nxt, i, lead))
        elif nxt:
            for name in ("K", "Q", "V"):
                if (j, hh) == self.at[name]:
                    ev.append((name, nxt, 0, 0))
            for name, at in (("Q", (5, 2)), ("K", (7, 2))):
                if (j, hh) == at:
                    ev.append((name, nxt, 0, 1))
        for after, slot, name in ((2, 3, "ctx_T"), (3, 2, "out_proj"), (4, 3, "x_T")):
            t = self.earlier(i, j, after, main, prev)
            if t and hh == slot and t[2] % 4 == 3:
                ev.append((name,) + t)
        return ev

    def count(self, i, main, nxt, prev):
        return sum(len(self.events(i, j, hh, main, nxt, prev)) for j in range(self.G) for hh in range(4))

    def x_start(self, i):
        if isinstance(i, int):
            return self.x_before[i]
        full = self.x_before[2] - self.x_before[1]
        return i * full + (self.x_before[1] - full)

    def slots_of_step(self, i, main, nxt, prev):
        x, n = self.x_start(i), 0
        for j in range(self.G):
            for hh in range(4):
                evs = []
                for ev in self.events(i, j, hh, main, nxt, prev):
                    evs.append(ev + (x + n,))
                    n += 1
                yield j, hh, evs


def run_steps(eng, first, second, step):
    step(first, -1, False, first, None)
    step(first, 0, True, first, None)
    with eng.Fori(1, first.S - 1) as i:
        step(first, i, True, first, first)
    step(first, first.S - 1, True, second, first)
    step(second, 0, True, second, first)
    with eng.Fori(1, second.S - 2) as i:
        step(second, i, True, second, second)
    step(second, second.S - 2, True, second, second)
    step(second, second.S - 1, True, None, second)
    step(second, second.S, False, None, second)


def count_events(first, second, x):
    for ph, other in ((first, None), (second, first)):
        for i in range(-1 if ph is first else 0, ph.S + (ph is second)):
            ph.x_before[i] = x
            nxt = ph if i < ph.S - 1 else second if ph is first else None
            x += ph.count(i, 0 <= i < ph.S, nxt, None if i < 0 else ph if i > 0 else other)
    return x


def run_blocks(eng, block):
    block(0)
    with eng.Fori(1, 4) as tb:
        block(tb)


def wait(eng, sem, value):
    if not isinstance(value, int) or value > 0:
        eng.wait_ge(sem, value)


def decoder_layer(nc, x_tok_d, kvT_d, wdkvT_d, wuk_d, wuv_d, self_wq_d, self_wo_d,
                  cross_wq_d, cross_wk_d, cross_wv_d, cross_wo_d, wg_d, w1_d, w2_d, out_d):
    SELF = Phase(0, True, T, 2, 3, 0, 0, 0, 0, 0)
    items, units, banks = B * 4, B * 4 * SELF.UN, B * 4 * SELF.MB
    CROSS = Phase(1, False, TC, 1, 2, items, units, banks, SELF.S, B)
    XN = count_events(SELF, CROSS, 1)
    ALL_UNITS, ALL_BANKS = units + B * 4 * CROSS.UN, banks + B * 4 * CROSS.MB

    ctx = ExitStack()
    with ctx:
        def sb(name, shape, dt=F32):
            return ctx.enter_context(nc.sbuf_tensor(name, shape, dt))

        def pb(name, shape):
            return ctx.enter_context(nc.psum_tensor(name, shape, F32))

        def sem(name):
            return ctx.enter_context(nc.semaphore(name))

        x_tok = sb("x_tok", [P, NT, D])
        xT = sb("xT", [P, B * T])
        kvT = sb("kvT", [P, KV])
        w_self = sb("w_self", [P, 4, D])
        w_cross = sb("w_cross", [P, 4, D])
        w_lat = sb("w_lat", [32, 3, D])
        w_gate = sb("w_gate", [P, E])
        w1 = sb("w1", [P, E, HID])
        w2 = sb("w2", [P, E, 2, D])
        ident = sb("ident", [P, P])
        ident_b = sb("ident_b", [P, P], BF16)
        mask_b = sb("mask_b", [P, P], BF16)
        k_parts = sb("k_parts", [P, 2, KV], F32R)
        q_parts = sb("q_parts", [P, 2, KV], F32R)
        k_stack = sb("k_stack", [P, 8192], F32R)
        q_stack = sb("q_stack", [P, 8192], F32R)
        probs = sb("probs", [P, 2, 4096])
        v_new = sb("v_new", [P, KV // P, D])
        v_aug = sb("v_aug", [P, KV // P, H, VW])
        mx = sb("mx", [P, 2, QT, 4])
        mx_row = sb("mx_row", [4, 2, T], F32R)
        u_sb = sb("u_sb", [P, T])
        rden = sb("rden", [P, QT, 4])
        ctxn = sb("ctxn", [P, QT, D])
        ctxT = sb("ctxT", [P, T])
        y_sb = sb("y_sb", [P, 4, D])
        xn = sb("xn", [P, QT, D])
        stats = sb("stats", [P, 4, 6])
        mv = sb("mv", [P, 4, 2])
        rstd = sb("rstd", [P, 4])
        minus_half = sb("minus_half", [P, 4])
        relu = sb("relu", [P, 2, 2, 512])
        act2 = sb("act2", [P, 2, 2, 512])
        lg_sb = sb("lg_sb", [E, 512])
        lmax = sb("lmax", [P, 4])
        lsub = sb("lsub", [P, 4, E])
        lexp = sb("lexp", [P, 4, E])
        lsum = sb("lsum", [P, 4])
        lrec = sb("lrec", [P, 4])
        gp = sb("gp", [P, 4, 2 * E])
        top = sb("top", [P, 4, E])
        rest = sb("rest", [P, 4, 2 * E])
        comb = sb("comb", [P, 4, E])
        acc = sb("acc", [P, 4, D])
        res = sb("res", [P, 4, D])

        ps_s = pb("ps_s", [P, 2, 1024])
        ps_m = pb("ps_m", [P, 2, 512])
        ps_u = pb("ps_u", [P, 512])
        ps_x = pb("ps_x", [P, 512])

        k_scr = [nc.dram_tensor("k_scr_s", (SELF.S, 4, P, KV), F32).ap(),
                 nc.dram_tensor("k_scr_c", (CROSS.S, 4, P, KV), F32).ap()]
        q_scr = [nc.dram_tensor("q_scr_s", (SELF.S, 4, P, SELF.qcols), F32).ap(),
                 nc.dram_tensor("q_scr_c", (CROSS.S, 4, P, CROSS.qcols), F32).ap()]

        kv_loaded = sem("kv_loaded")
        taken = sem("taken")
        x_loaded = sem("x_loaded")
        lat_loaded = sem("lat_loaded")
        w_loaded = sem("w_loaded")
        ffn_loaded = sem("ffn_loaded")
        init_done = sem("init_done")
        q_stack_zero = sem("q_stack_zero")
        const_done = sem("const_done")
        qk_done = sem("qk_done")
        exp_done = sem("exp_done")
        masked = sem("masked")
        max_done = sem("max_done")
        max_read = sem("max_read")
        q_row_zero = sem("q_row_zero")
        mx_loaded = [sem(f"mx_loaded{p}") for p in range(2)]
        pv_done = sem("pv_done")
        u_read = sem("u_read")
        u_turned, u_divided = sem("u_turned"), sem("u_divided")
        x_full = sem("x_full")
        x_read = sem("x_read")
        k_hi, q_hi = sem("k_hi"), sem("q_hi")
        k_spilled, q_spilled = sem("k_spilled"), sem("q_spilled")
        stack_loaded = [[sem(f"stack{n}_{s}") for s in range(ph.slots)] for n, ph in enumerate((SELF, CROSS))]
        v_spread = sem("v_spread")
        rden_done = sem("rden_done")
        ln_chain = sem("ln_chain")
        mv_ready = sem("mv_ready")
        rstd_chain = sem("rstd_chain")
        x_new = sem("x_new")
        lg_done, lg_read, lt_done, lt_sub, lt_exp = (sem("lg_done"), sem("lg_read"), sem("lt_done"),
                                                     sem("lt_sub"), sem("lt_exp"))
        gate_chain = sem("gate_chain")
        h_done, relu_done, sq_done = sem("h_done"), sem("relu_done"), sem("sq_done")
        y_done, acc_chain = sem("y_done"), sem("acc_chain")
        fin_chain, fin_mv, fin_rstd = sem("fin_chain"), sem("fin_mv"), sem("fin_rstd")
        fin_done = sem("fin_done")
        stored = sem("stored")

        def apart(eng):
            eng.sem_inc(taken, 1)

        W = {SELF: w_self, CROSS: w_cross}

        def k_view(ph, slot_item, hh):
            n = (4 * slot_item + hh) * ph.keys
            return k_stack[:, n:n + ph.keys]

        def q_view(ph, slot_item, hh, q0=0, q1=T):
            n = (4 * slot_item + hh) * T
            return q_stack[:, n + q0:n + q1]

        block = ctx.enter_context(nc.Block())

        @block.sync
        def _(sp):
            sp.dma_start(w_lat[:, 0, :], wdkvT_d).then_inc(lat_loaded, 16)
            sp.dma_start(w_lat[:, 1, :], wuk_d).then_inc(lat_loaded, 16)
            sp.dma_start(w_lat[:, 2, :], wuv_d).then_inc(lat_loaded, 16)
            sp.dma_start(kvT[:, :], kvT_d[0]).then_inc(kv_loaded, 16)

            def step(ph, i, main, nxt, prev):
                for j, hh, evs in ph.slots_of_step(i, main, nxt, prev):
                    for name, eph, ei, arg, x in evs:
                        if name == "max_T":
                            sp.wait_ge(x_read, x + 1)
                            c = (arg % eph.G) * 4 * T
                            sp.dma_start(q_stack[ROW_M:ROW_M + 1, c:c + 4 * T].bitcast(F32),
                                         mx_row[:, arg % 2, :].bitcast(F32)).then_inc(mx_loaded[arg % 2], 16)
                        if name in ("K", "Q"):
                            sp.wait_ge(x_read, x + 1)
                            apart(sp)
                            scr = (k_scr if name == "K" else q_scr)[eph.n][ei + arg]
                            parts, cols = (k_parts, KV) if name == "K" else (q_parts, eph.qcols)
                            order = "(rep hl) p k -> rep p hl k" if name == "K" else "(hl rep) p k -> rep p hl k"
                            dst = scr.rearrange(order, rep=2)
                            for rep in range(2):
                                sp.dma_start(dst[rep], parts[:, :, 0:cols].bitcast(F32))\
                                  .then_inc(k_spilled if name == "K" else q_spilled, 16)
                        if name == "V" and not (eph is CROSS and isinstance(ei, int) and ei + arg == CROSS.S - 1):
                            sp.wait_ge(x_full, x + 1)
                            apart(sp)
                            sp.dma_start(kvT[:, :], kvT_d[ei + (arg + eph.step0 + 1)]).then_inc(kv_loaded, 16)
                    if nxt and (j, hh) in ph.load_at:
                        slot = ph.load_at.index((j, hh))
                        nph, ni = (ph, i + 1) if nxt is ph else (nxt, 0)
                        if main:
                            sp.wait_ge(qk_done, ph.units(i, (slot + 1) * (ph.G // ph.slots)))
                            apart(sp)
                        elif slot == 0:
                            sp.wait_ge(const_done, 1)
                            sp.wait_ge(q_stack_zero, 1)
                        if slot == 0:
                            sp.wait_ge(k_spilled, (i + (2 + ph.step0)) * 32)
                            sp.wait_ge(q_spilled, (i + (2 + ph.step0)) * 32)
                            apart(sp)
                        for scr, stack, width in ((k_scr, k_stack, nph.keys), (q_scr, q_stack, T)):
                            if nph is SELF:
                                bb, h0 = slot // 2, (slot % 2) * 8
                                cols = 8 * width
                                src = scr[0][ni].rearrange("r (d h) k -> (r d) h k", d=HD)\
                                    [:, h0:h0 + 8, bb * width:(bb + 1) * width]
                            else:
                                cols = 4 * width
                                src = scr[1][ni, :, 32 * slot:32 * slot + 32, :]\
                                    .rearrange("r (d h) k -> r d (h k)", d=HD)
                            sp.dma_start(stack[0:4 * HD, slot * cols:(slot + 1) * cols].bitcast(F32), src)\
                              .then_inc(stack_loaded[nph.n][slot], 16)

            run_steps(sp, SELF, CROSS, step)
            out_v = out_d.rearrange("(b t p) d -> b p t d", t=4, p=P)
            with sp.Fori(0, 4) as tb:
                sp.wait_ge(fin_done, tb * 4 + 4)
                apart(sp)
                sp.dma_start(out_v[tb], res[:, :, :]).then_inc(stored, 16)
            sp.wait_ge(stored, 16 * 4)

        @block.gpsimd
        def _(pool):
            pool.memset(ident[:, :], 0.0).then_inc(init_done, 1)
            pool.memset(ident_b[:, :], 0.0).then_inc(init_done, 1)
            pool.memset(mask_b[:, :], 0.0).then_inc(init_done, 1)
            pool.memset(k_stack[:, :].bitcast(F32), 0.0).then_inc(init_done, 1)
            pool.memset(v_aug[:, :, :, :].rearrange("p a b c -> p (a b c)"), 0.0).then_inc(init_done, 1)
            pool.wait_ge(init_done, 5)
            for m in (ident, ident_b):
                pool.affine_select(out=m[:, :], in_=m[:, :], compare_op=ALU.not_equal, fill=1.0, base=0,
                                   pattern=[[-1, P]], channel_multiplier=1).then_inc(init_done, 1)
            pool.affine_select(out=mask_b[:, :], in_=mask_b[:, :], compare_op=ALU.is_ge, fill=MASKED, base=0,
                               pattern=[[-1, P]], channel_multiplier=1).then_inc(init_done, 1)
            pool.memset(v_aug[:, :, :, HD:HD + 1].rearrange("p a b c -> p (a b c)"), 1.0).then_inc(init_done, 1)
            pool.memset(gp[:, :, E:2 * E], -1.0).then_inc(init_done, 1)
            pool.memset(minus_half[:, :], -0.5).then_inc(init_done, 1)
            pool.wait_ge(init_done, 11)
            pool.memset(k_stack[ROW_M:ROW_M + 1, :].bitcast(F32), -1.0).then_inc(init_done, 1)
            pool.wait_ge(init_done, 12)
            pool.memset(top[:, :, :], -1.0).then_inc(const_done, 1)

            def normalise(y, out, tiles, chain, base, done):
                apart(pool)
                pool.tensor_scalar(rstd[:, 0:tiles], mv[:, 0:tiles, 1], LN_EPS, 1.0, ALU.add, ALU.mult)\
                    .then_inc(chain, 1)
                pool.wait_ge(chain, base + 1)
                pool.tensor_tensor(rstd[:, 0:tiles], rstd[:, 0:tiles], minus_half[:, 0:tiles], ALU.pow)\
                    .then_inc(chain, 1)
                pool.wait_ge(chain, base + 2)
                apart(pool)
                for t in range(tiles):
                    pool.tensor_scalar(out[:, t, :], y[:, t, :], mv[:, t, 0:1], rstd[:, t:t + 1],
                                       ALU.subtract, ALU.mult).then_inc(done, 1)

            def step(ph, i, main, nxt, prev):
                for j in range(ph.G):
                    w = ph.item(i, j)
                    if j == 0 and main:
                        pool.wait_ge(x_read, ph.x_start(i))
                        wait(pool, pv_done, w)
                        apart(pool)
                        pool.tensor_scalar(v_aug[:, :, :, 0:HD],
                                           v_new[:, :, :].rearrange("p c (h d) -> p c h d", d=HD),
                                           1.0, 0.0, ALU.mult, ALU.add).then_inc(v_spread, 1)
                        pool.wait_ge(v_spread, i + (ph.step0 + 1))
                    if main and ph.causal:
                        pool.wait_ge(exp_done, ph.units(i, j + 1))
                        apart(pool)
                        pr = probs[:, j % 2, 0:2048].rearrange("p (b q) -> p b q", q=256)[:, :, 0:P]
                        pool.affine_select(out=pr, in_=pr, compare_op=ALU.is_ge, fill=0.0, base=0,
                                           pattern=[[0, 8], [1, P]], channel_multiplier=-1)\
                            .then_inc(masked, 1)
                    if main:
                        pool.wait_ge(qk_done, ph.units(i, j + 1))
                        apart(pool)
                        if ph.causal:
                            pool.wait_ge(masked, w + 1)
                            apart(pool)
                        c = j * 4 * T
                        pool.memset(q_stack[ROW_M:ROW_M + 1, c:c + 4 * T].bitcast(F32), 0.0).then_inc(q_row_zero, 1)
                        pool.wait_ge(q_row_zero, w + 1)
                    last = ph.earlier(i, j, 3, main, prev)
                    if last and last[2] % 4 == 3:
                        bph, bi, bj = last
                        bn = bi * bph.bps + (bph.batch0 + bj // 4)
                        pool.wait_ge(mv_ready, bn + 1)
                        normalise(y_sb, xn, QT, rstd_chain, bn * 2, x_new)
                        pool.wait_ge(x_new, bn * QT + QT)

            run_steps(pool, SELF, CROSS, step)

            def block_(tb):
                for e in range(E):
                    n = tb * (2 * E) + 2 * e
                    for c in range(2):
                        pool.wait_ge(relu_done, n + (c + 1))
                        wait(pool, y_done, tb * E + (e - 1))
                        pool.tensor_tensor(act2[:, e % 2, c, :], relu[:, e % 2, c, :], relu[:, e % 2, c, :],
                                           ALU.mult).then_inc(sq_done, 1)
                pool.wait_ge(fin_mv, tb * 4 + 4)
                wait(pool, stored, tb * 16)
                normalise(acc, res, 4, fin_rstd, tb * 2, fin_done)

            run_blocks(pool, block_)

        @block.scalar
        def _(act):
            def copy(out, in_):
                return nc.scalar.activation(out, in_, ACT.Copy)

            act.dma_start(w_self[:, 0, :], self_wq_d).then_inc(w_loaded, 16)
            act.dma_start(w_self[:, 3, :], self_wo_d).then_inc(w_loaded, 16)
            act.dma_start(x_tok[:, :, :], x_tok_d.rearrange("(t p) d -> p t d", p=P)).then_inc(x_loaded, 16)
            for n, d in enumerate((cross_wq_d, cross_wk_d, cross_wv_d, cross_wo_d)):
                act.dma_start(w_cross[:, n, :], d).then_inc(w_loaded, 16)
            act.dma_start(w_gate[:, :], wg_d).then_inc(ffn_loaded, 16)
            act.dma_start(w1[:, :, :], w1_d).then_inc(ffn_loaded, 16)
            act.dma_start(w2[:, :, :, :], w2_d).then_inc(ffn_loaded, 16)
            act.wait_ge(x_full, 1)
            copy(w_self[:, 1:3, :].rearrange("p a b -> p (a b)"), ps_x[:, 0:2 * D]).then_inc(x_read, 1)

            def step(ph, i, main, nxt, prev):
                for j, hh, evs in ph.slots_of_step(i, main, nxt, prev):
                    w = ph.item(i, j)
                    if main and hh % ph.UH == 0:
                        u = hh // ph.UH
                        act.wait_ge(qk_done, ph.units(i, j) + (u + 1))
                        if hh == 0:
                            wait(act, pv_done, w - 1)
                        if ph.causal:
                            nc.scalar.activation(
                                probs[:, j % 2, u * 1024:u * 1024 + 1024]
                                .rearrange("p (h c) -> p h c", h=2)[:, :, 0:384],
                                ps_s[:, u % 2, :].rearrange("p (h c) -> p h c", h=2)[:, :, 0:384],
                                ACT.Exp, scale=SCALE).then_inc(exp_done, 1)
                        else:
                            nc.scalar.activation(probs[:, j % 2, hh * 1024:hh * 1024 + 1024], ps_s[:, u % 2, :],
                                                 ACT.Exp, scale=SCALE).then_inc(exp_done, 1)
                    if hh == 3 and ph.earlier(i, j, 1, main, prev):
                        act.wait_ge(pv_done, w)
                        wait(act, u_turned, w - 1)
                        copy(u_sb[:, :], ps_u[:, 0:T]).then_inc(u_read, 1)
                    for name, eph, ei, arg, x in evs:
                        if name in ("max_T", "K", "Q", "V", "ctx_T", "x_T"):
                            act.wait_ge(x_full, x + 1)
                        if name == "max_T":
                            copy(mx_row[:, arg % 2, :], ps_x[0:4, 0:T]).then_inc(x_read, 1)
                        if name == "K":
                            wait(act, k_spilled, ei * 32 + 32 * (arg + eph.step0))
                            copy(k_parts[:, 0, :], ps_x[:, 0:KV]).then_inc(k_hi, 1)
                        if name == "Q":
                            wait(act, q_spilled, ei * 32 + 32 * (arg + eph.step0))
                            copy(q_parts[:, 0, 0:eph.qcols], ps_x[:, 0:eph.qcols]).then_inc(q_hi, 1)
                        if name == "V":
                            wait(act, v_spread, ei + (arg + eph.step0))
                            copy(v_new[:, :, :].rearrange("p c n -> p (c n)"), ps_x[:, 0:KV]).then_inc(x_read, 1)
                        if name == "ctx_T":
                            copy(ctxT[:, :], ps_x[:, 0:T]).then_inc(x_read, 1)
                        if name == "x_T":
                            b = ei * eph.bps + arg // 4
                            copy(x_tok[:, bass.ds(b * QT, QT), :], xn[:, :, :])
                            copy(xT[:, bass.ds(b * T, T)], ps_x[:, 0:T]).then_inc(x_read, 1)

            run_steps(act, SELF, CROSS, step)

            def block_(tb):
                act.wait_ge(lg_done, tb + 1)
                wait(act, lt_done, tb)
                copy(lg_sb[:, :], ps_x[0:E, 0:512]).then_inc(lg_read, 1)
                for e in range(E):
                    if e == 1:
                        act.wait_ge(lt_sub, tb + 1)
                        nc.scalar.activation(lexp[:, :, :], lsub[:, :, :], ACT.Exp).then_inc(lt_exp, 1)
                    for c in range(2):
                        n = tb * (2 * E) + (2 * e + c)
                        act.wait_ge(h_done, n + 1)
                        wait(act, sq_done, n - 3)
                        nc.scalar.activation(relu[:, e % 2, c, :], ps_s[:, e % 2, 512 * c:512 * c + 512],
                                             ACT.Relu).then_inc(relu_done, 1)

            run_blocks(act, block_)

        @block.vector
        def _(dve):
            v = nc.vector
            v.memset(q_stack[:, :].bitcast(F32), 0.0).then_inc(q_stack_zero, 1)
            dve.wait_ge(x_loaded, 16)

            def moments(y, tiles, chain, base, done):
                for t in range(tiles):
                    v.bn_stats(stats[:, t, :], y[:, t, :]).then_inc(chain, 1)
                dve.wait_ge(chain, base + tiles)
                apart(dve)
                for t in range(tiles):
                    done(t, v.bn_aggr(mv[:, t, :], stats[:, t, :]))

            def divide(w, item):
                dve.wait_ge(u_turned, w - 1)
                g = item[2] % 4
                u = ps_u[:, T:2 * T].rearrange("p (t h c) -> p t h c", t=QT, c=VW)
                v.reciprocal(rden[:, :, :], u[:, :, :, HD]).then_inc(rden_done, 1)
                dve.wait_ge(rden_done, w - 1)
                o = ctxn[:, :, 32 * g:32 * g + 32].rearrange("p t (h c) -> p t h c", c=HD)
                v.tensor_tensor(o, u[:, :, :, 0:HD], rden[:, :, :, None].broadcast_to([P, QT, 4, HD]),
                                ALU.mult).then_inc(u_divided, 1)

            def step(ph, i, main, nxt, prev):
                for j, hh, evs in ph.slots_of_step(i, main, nxt, prev):
                    w = ph.item(i, j)
                    t_item = ph.later(i, j, 0, main, nxt)
                    if t_item:
                        tph, ti, tj = t_item
                        if tph.causal:
                            dve.wait_ge(max_done, tph.banks(ti, tj) + (hh + 1))
                            v.tensor_reduce(out=mx[:, tj % 2, 0, hh:hh + 1], in_=ps_m[:, hh % 2, 0:P],
                                            axis=AX.X, op=ALU.max)
                            v.tensor_reduce(out=mx[:, tj % 2, 1, hh:hh + 1], in_=ps_m[:, hh % 2, P:3 * P],
                                            axis=AX.X, op=ALU.max).then_inc(max_read, 1)
                        else:
                            dve.wait_ge(max_done, tph.banks(ti, tj) + (2 * hh + 1))
                            v.tensor_reduce(out=mx[:, tj % 2, 0, hh:hh + 1], in_=ps_m[:, 0, :],
                                            axis=AX.X, op=ALU.max).then_inc(max_read, 1)
                    two_ago = ph.earlier(i, j, 2, main, prev)
                    if hh == 0 and two_ago:
                        divide(w, two_ago)
                    if t_item and not tph.causal:
                        dve.wait_ge(max_done, tph.banks(ti, tj) + (2 * hh + 2))
                        v.tensor_reduce(out=mx[:, tj % 2, 1, hh:hh + 1], in_=ps_m[:, 1, :],
                                        axis=AX.X, op=ALU.max).then_inc(max_read, 1)
                    for name, eph, ei, arg, x in evs:
                        if name in ("K", "Q"):
                            dve.wait_ge(k_hi if name == "K" else q_hi, ei + (arg + eph.step0 + 1))
                            parts, cols = (k_parts, KV) if name == "K" else (q_parts, eph.qcols)
                            v.tensor_tensor(parts[:, 1, 0:cols], ps_x[:, 0:cols],
                                            parts[:, 0, 0:cols].bitcast(F32), ALU.subtract).then_inc(x_read, 1)
                        if name == "out_proj":
                            dve.wait_ge(x_full, x + 1)
                            b = ei * eph.bps + arg // 4
                            bn = ei * eph.bps + (eph.batch0 + arg // 4)
                            wait(dve, x_new, bn * QT)
                            v.tensor_tensor(y_sb[:, 0:QT, :],
                                            ps_x[:, 0:T].rearrange("p (t d) -> p t d", t=QT),
                                            x_tok[:, bass.ds(b * QT, QT), :], ALU.add).then_inc(x_read, 1)
                            dve.wait_ge(x_read, x + 1)

                            def done(t, ins):
                                if t == QT - 1:
                                    ins.then_inc(mv_ready, 1)
                            moments(y_sb, QT, ln_chain, bn * QT, done)

            run_steps(dve, SELF, CROSS, step)

            def block_(tb):
                g0 = tb * GATE

                def link(ins, n):
                    ins.then_inc(gate_chain, 1)
                    dve.wait_ge(gate_chain, g0 + n)
                    apart(dve)

                def acc_expert(e):
                    dve.wait_ge(y_done, tb * E + (e + 1))
                    for t in range(4):
                        src = x_tok[:, bass.ds(tb * 4 + t, 1), :].rearrange("p a d -> p (a d)") if e == 0 \
                            else acc[:, t, :]
                        v.scalar_tensor_tensor(acc[:, t, :], ps_m[:, e % 2, t * D:(t + 1) * D],
                                               comb[:, t, e:e + 1], src, op0=ALU.mult, op1=ALU.add)\
                            .then_inc(acc_chain, 1)

                dve.wait_ge(lt_done, tb + 1)
                lt = ps_u[:, 0:4 * E].rearrange("p (t e) -> p t e", t=4)
                link(v.tensor_reduce(out=lmax[:, :], in_=lt, axis=AX.X, op=ALU.max), 1)
                v.tensor_tensor(lsub[:, :, :], lt, lmax[:, :, None].broadcast_to([P, 4, E]),
                                ALU.subtract).then_inc(lt_sub, 1)
                dve.wait_ge(lt_exp, tb + 1)
                link(v.tensor_reduce(out=lsum[:, :], in_=lexp[:, :, :], axis=AX.X, op=ALU.add), 2)
                link(v.reciprocal(lrec[:, :], lsum[:, :]), 3)
                link(v.tensor_tensor(gp[:, :, 0:E], lexp[:, :, :], lrec[:, :, None].broadcast_to([P, 4, E]),
                                     ALU.mult), 4)
                for t in range(4):
                    v.max(out=rest[:, t, 0:E], in_=gp[:, t, 0:E]).then_inc(gate_chain, 1)
                dve.wait_ge(gate_chain, g0 + 8)
                link(v.tensor_copy(top[:, :, 0:2], rest[:, :, 0:2]), 9)
                link(v.scalar_tensor_tensor(lsum[:, :], top[:, :, 0], TOPW_EPS, top[:, :, 1],
                                            op0=ALU.add, op1=ALU.add), 10)
                link(v.reciprocal(lrec[:, :], lsum[:, :]), 11)
                for t in range(4):
                    v.match_replace(out=rest[:, t, :], in_to_replace=top[:, t, :], in_values=gp[:, t, :],
                                    imm_value=0.0).then_inc(gate_chain, 1)
                dve.wait_ge(gate_chain, g0 + 15)
                link(v.tensor_tensor(comb[:, :, :], gp[:, :, 0:E], rest[:, :, 0:E], ALU.subtract), 16)
                link(v.tensor_tensor(comb[:, :, :], comb[:, :, :], lrec[:, :, None].broadcast_to([P, 4, E]),
                                     ALU.mult), 17)
                for e in range(E):
                    if e > 0:
                        dve.wait_ge(acc_chain, tb * (4 * E) + 4 * e)
                    else:
                        wait(dve, fin_done, tb * 4)
                    acc_expert(e)
                dve.wait_ge(acc_chain, tb * (4 * E) + 4 * E)

                def done(t, ins):
                    ins.then_inc(fin_mv, 1)
                moments(acc, 4, fin_chain, tb * 4, done)

            run_blocks(dve, block_)

        @block.tensor
        def _(pe):
            mm = nc.tensor.matmul
            pe.wait_ge(lat_loaded, 48)
            for n in range(2):
                last = mm(ps_x[:, n * D:(n + 1) * D], w_lat[:, 0, :], w_lat[:, 1 + n, :], start=True, stop=True)
            last.then_inc(x_full, 1)
            pe.wait_ge(const_done, 1)

            def step(ph, i, main, nxt, prev):
                for j, hh, evs in ph.slots_of_step(i, main, nxt, prev):
                    w = ph.item(i, j)
                    if main and hh % ph.UH == 0:
                        u = hh // ph.UH
                        if hh == 0:
                            pe.wait_ge(mx_loaded[j % 2], i * (8 * ph.G) + 16 * ((ph.item0 + j) // 2 + 1))
                        wait(pe, exp_done, ph.units(i, j) + (u - 1))
                        for h in range(hh, hh + ph.UH):
                            for c in range(ph.KC):
                                q0 = c * P if ph.causal else 0
                                col = (h - hh) * 512 + c * T
                                last = mm(ps_s[:, u % 2, col:col + T - q0],
                                          k_view(ph, j, h)[:, c * P:(c + 1) * P], q_view(ph, j, h, q0, T),
                                          start=True, stop=True)
                        last.then_inc(qk_done, 1)
                    t_item = ph.later(i, j, 0, main, nxt)
                    if t_item:
                        tph, ti, tj = t_item
                        local = tj % tph.G
                        if hh == 0:
                            pe.wait_ge(stack_loaded[tph.n][local // (tph.G // tph.slots)],
                                       ti * 32 + 32 * (tj // tph.G + 1))
                            before = SELF.G if isinstance(ti, int) and ti + tj // tph.G == 0 else tph.G
                            wait(pe, q_row_zero, tph.item(ti, tj) + (1 - before))
                        kv = k_view(tph, local, hh)
                        if tph.causal:
                            wait(pe, max_read, tph.banks(ti, tj) + (hh - 1))
                            m = ps_m[:, hh % 2, 0:512].rearrange("p (b q) -> p b q", q=256)[:, :, 0:P]
                            mm(ps_m[:, hh % 2, 0:P], q_view(tph, local, hh, 0, P), kv[:, 0:P],
                               start=True, stop=False)
                            mm(ps_m[:, hh % 2, P:3 * P], q_view(tph, local, hh, P, T), kv, start=False, stop=False)
                            mm(m, ident_b[:, :], mask_b[:, None, :].broadcast_to([P, 2, P]),
                               start=False, stop=True).then_inc(max_done, 1)
                        else:
                            wait(pe, max_read, tph.banks(ti, tj) + (2 * hh - 1))
                            mm(ps_m[:, 0, :], q_view(tph, local, hh, 0, P), kv,
                               start=True, stop=True).then_inc(max_done, 1)
                    if hh == 0 and ph.earlier(i, j, 2, main, prev):
                        pe.wait_ge(u_read, w - 1)
                        for t in range(QT):
                            last = nc.tensor.transpose(ps_u[:, T + t * P:T + (t + 1) * P],
                                                       u_sb[:, t * P:(t + 1) * P], ident[:, :])
                        last.then_inc(u_turned, 1)
                    done = ph.earlier(i, j, 1, main, prev)
                    if done:
                        pph, pi, pj = done
                        chunks = pph.pv_chunks[hh]
                        if 0 in chunks:
                            if pph.causal:
                                pe.wait_ge(masked, w)
                            else:
                                pe.wait_ge(exp_done, pph.units(pi, pj + 1))
                            pe.wait_ge(v_spread, pi + (pph.step0 + pj // pph.G + 1))
                            wait(pe, u_read, w - 1)
                            wait(pe, u_divided, w - 1)
                        for c in chunks:
                            g, c0 = pj % 4, (pj % pph.G // 4) * pph.KC
                            for h in range(4):
                                q0 = c * P if pph.causal else 0
                                col = h * (512 if pph.causal else 1024) + c * T
                                last = mm(ps_u[32 * h:32 * h + 32, q0:T], v_aug[:, c0 + c, 4 * g + h, :],
                                          probs[:, pj % 2, col:col + T - q0],
                                          start=(c == 0), stop=(c == pph.KC - 1))
                        if hh == 3:
                            last.then_inc(pv_done, 1)
                    if t_item and not tph.causal:
                        wait(pe, max_read, tph.banks(ti, tj) + 2 * hh)
                        mm(ps_m[:, 1, :], q_view(tph, local, hh, P, T), kv,
                           start=True, stop=True).then_inc(max_done, 1)
                    for name, eph, ei, arg, x in evs:
                        wait(pe, x_read, x)
                        if name == "max_T":
                            pe.wait_ge(max_read, eph.banks(ei, arg + 1))
                            for t in range(QT):
                                last = nc.tensor.transpose(ps_x[0:4, t * P:(t + 1) * P], mx[:, arg % 2, t, :],
                                                           ident[:, :])
                        if name == "K":
                            pe.wait_ge(kv_loaded, ei * 16 + 16 * (arg + eph.step0 + 1))
                            last = mm(ps_x[:, 0:KV], W[eph][:, 1, :], kvT[:, :], start=True, stop=True)
                        if name == "Q":
                            if eph is SELF:
                                if isinstance(ei, int) and ei < 0:
                                    pe.wait_ge(w_loaded, 16 * 6)
                                src = kvT[:, :]
                            elif isinstance(ei, int):
                                src = xT[:, (ei + arg) * T:(ei + arg + 1) * T]
                            else:
                                src = xT[:, bass.ds((ei + arg) * T, T)]
                            last = mm(ps_x[:, 0:eph.qcols], W[eph][:, 0, :], src, start=True, stop=True)
                        if name == "V":
                            for c in range(KV // P):
                                last = mm(ps_x[:, c * D:(c + 1) * D], kvT[:, c * P:(c + 1) * P], W[eph][:, 2, :],
                                          start=True, stop=True)
                        if name == "ctx_T":
                            pe.wait_ge(u_divided, eph.item(ei, arg) + 1)
                            for t in range(QT):
                                last = nc.tensor.transpose(ps_x[:, t * P:(t + 1) * P], ctxn[:, t, :], ident[:, :])
                        if name == "out_proj":
                            for t in range(QT):
                                last = mm(ps_x[:, t * D:(t + 1) * D], ctxT[:, t * P:(t + 1) * P], W[eph][:, 3, :],
                                          start=True, stop=True)
                        if name == "x_T":
                            pe.wait_ge(x_new, ei * (QT * eph.bps) + QT * (eph.batch0 + arg // 4 + 1))
                            for t in range(QT):
                                last = nc.tensor.transpose(ps_x[:, t * P:(t + 1) * P], xn[:, t, :], ident[:, :])
                        last.then_inc(x_full, 1)

            run_steps(pe, SELF, CROSS, step)

            pe.wait_ge(ffn_loaded, 48)
            pe.wait_ge(x_read, XN)
            pe.wait_ge(exp_done, ALL_UNITS)
            pe.wait_ge(max_read, ALL_BANKS)

            def block_(tb):
                toks = xT[:, bass.ds(tb * 512, 512)]

                def second(e):
                    wait(pe, acc_chain, tb * (4 * E) + 4 * (e - 1))
                    pe.wait_ge(sq_done, tb * (2 * E) + (2 * e + 2))
                    for t in range(4):
                        for c in range(2):
                            last = mm(ps_m[:, e % 2, t * D:(t + 1) * D], act2[:, e % 2, c, t * P:(t + 1) * P],
                                      w2[:, e, c, :], start=(c == 0), stop=(c == 1))
                    last.then_inc(y_done, 1)

                wait(pe, lg_read, tb)
                mm(ps_x[0:E, 0:512], w_gate[:, :], toks, start=True, stop=True).then_inc(lg_done, 1)
                for e in range(E):
                    for c in range(2):
                        wait(pe, relu_done, tb * (2 * E) + (2 * e + c - 3))
                        mm(ps_s[:, e % 2, 512 * c:512 * c + 512], w1[:, e, c * P:(c + 1) * P], toks,
                           start=True, stop=True).then_inc(h_done, 1)
                    if e == 0:
                        pe.wait_ge(lg_read, tb + 1)
                        wait(pe, lt_sub, tb)
                        apart(pe)
                        for t in range(4):
                            last = nc.tensor.transpose(ps_u[:, t * E:(t + 1) * E], lg_sb[:, t * P:(t + 1) * P],
                                                       ident[0:E, 0:E])
                        last.then_inc(lt_done, 1)
                    if e > 0:
                        second(e - 1)
                second(E - 1)

            run_blocks(pe, block_)


def kernel(x, ctx_1024, L0_attn_W_DKV, L0_attn_W_UK, L0_attn_W_UV, L0_attn_W_UQ, L0_attn_W_O,
           L0_xattn_w_q, L0_xattn_w_k, L0_xattn_w_v, L0_xattn_w_o, L0_ffn_Wg, L0_ffn_W1, L0_ffn_W2):
    import numpy as np
    import concourse.bacc as bacc
    from concourse.bass_utils import run_bass_kernel_spmd

    a = {n: np.asarray(v) for n, v in locals().items() if n[0] in "xcL"}
    x, ctx_kv = a["x"], a["ctx_1024"]
    by_dim = np.arange(D).reshape(H, HD).T.reshape(-1)
    by_group = np.arange(D).reshape(4, 4, HD).transpose(0, 2, 1).reshape(-1)
    kvT = np.concatenate([x.reshape(B // 2, KV, D).transpose(0, 2, 1), ctx_kv.transpose(0, 2, 1)])
    arrays = {
        "x_tok": x.reshape(B * T, D),
        "kvT": kvT,
        "wdkvT": a["L0_attn_W_DKV"].T,
        "wuk": a["L0_attn_W_UK"][:, by_dim],
        "wuv": a["L0_attn_W_UV"],
        "self_wq": a["L0_attn_W_UQ"][:, by_dim],
        "self_wo": a["L0_attn_W_O"],
        "cross_wq": a["L0_xattn_w_q"].T[:, by_group],
        "cross_wk": a["L0_xattn_w_k"].T[:, by_group],
        "cross_wv": a["L0_xattn_w_v"].T,
        "cross_wo": a["L0_xattn_w_o"].T,
        "wg": a["L0_ffn_Wg"],
        "w1": a["L0_ffn_W1"].transpose(1, 0, 2),
        "w2": a["L0_ffn_W2"].reshape(E, 2, P, D).transpose(2, 0, 1, 3),
    }
    arrays = {f"{n}_dram": np.ascontiguousarray(v) for n, v in arrays.items()}
    nc = bacc.Bacc("TRN2", target_bir_lowering=False, num_devices=1)
    args = [nc.dram_tensor(n, v.shape, mybir.dt.from_np(v.dtype), kind="ExternalInput").ap()
            for n, v in arrays.items()]
    out = nc.dram_tensor("out_dram", (B * T, D), F32, kind="ExternalOutput").ap()
    decoder_layer(nc, *args, out)
    r = run_bass_kernel_spmd(nc, [arrays], core_ids=[0])
    return r.results[0]["out_dram"].reshape(B, T, D)
```

```python
from contextlib import ExitStack

import concourse.bass as bass
from concourse import mybir

F32 = mybir.dt.float32
F32R = mybir.dt.float32r
BF16 = mybir.dt.bfloat16
ALU = mybir.AluOpType
ACT = mybir.ActivationFunctionType
AX = mybir.AxisListType

P = 128
B, T, D = 8, 256, 128
TC = 512
H, HD = 16, 8
E, HID = 8, 256
QT = T // P
NT = B * QT
SCALE = float(HD) ** -0.5
LN_EPS = 1e-5
TOPW_EPS = 1e-8
BT = 4
BLOCKS = NT // BT
REST_AT = {0: (0, (0, 1, 2, 3)), 1: (1, (0,)), 3: (1, (1, 2, 3)), 4: (2, (0, 1, 2, 3)), 5: (3, (0,)),
           6: (3, (1, 2, 3))}
GATE_TILES = ((0, 12), (12, 16))
MASKED = -1e30
KV = 512
VW = 32
ROW_M = 4 * HD


class Phase:

    def __init__(self, n, causal, keys, batches_per_step, ahead, item0, unit0, bank0, step0, batch0):
        self.n, self.causal, self.keys = n, causal, keys
        self.KC = keys // P
        self.bps = batches_per_step
        self.ahead = ahead
        self.G = 4 * batches_per_step
        self.S = B // batches_per_step
        self.UH = 2 if causal else 1
        self.UN = 4 // self.UH
        self.MB = 4 if causal else 8
        self.item0, self.unit0, self.bank0, self.step0, self.batch0 = item0, unit0, bank0, step0, batch0
        self.qcols = T * batches_per_step
        self.slots = 4
        self.at = {"K": (0, 2), "Q": (1, 0), "V": (4, 3)} if causal else {"V": (1, 2), "Q": (3, 0), "K": (3, 2)}
        self.lead = {"K": 1, "Q": 1, "V": 1} if causal else {"V": 1, "Q": 2, "K": 2}
        self.load_at = [(2, 3), (3, 3), (5, 3), (7, 3)] if causal else [(0, 3), (1, 3), (2, 3), (3, 3)]
        self.pv_chunks = [(), (), (0,), (1,)] if causal else [(), (0,), (1,), (2, 3)]
        self.x_before = {}

    def item(self, i, j):
        return i * self.G + (self.item0 + j)

    def units(self, i, j):
        return i * (self.G * self.UN) + (self.unit0 + j * self.UN)

    def banks(self, i, j):
        return i * (self.G * self.MB) + (self.bank0 + j * self.MB)

    def later(self, i, j, less, main, nxt):
        t = j + self.ahead - less
        if t < self.G:
            return (self, i, t) if main else None
        if nxt is self:
            return self, i, t
        if nxt is not None and j + nxt.ahead - less >= self.G:
            return nxt, 0, j + nxt.ahead - less - self.G
        return None

    def earlier(self, i, j, back, main, prev):
        if j >= back:
            return (self, i, j - back) if main else None
        if prev is self:
            return self, i, j - back
        return (prev, prev.S - 1, j - back + prev.G) if prev else None

    def events(self, i, j, hh, main, nxt, prev):
        ev = []
        if hh == 1:
            t = self.later(i, j, 1, main, nxt)
            if t:
                ev.append(("max_T",) + t)
        if nxt is self:
            for name, lead in self.lead.items():
                if (j, hh) == self.at[name] and not (isinstance(i, int) and i + lead >= self.S):
                    ev.append((name, nxt, i, lead))
        elif nxt:
            for name in ("K", "Q", "V"):
                if (j, hh) == self.at[name]:
                    ev.append((name, nxt, 0, 0))
            for name, at in (("Q", (5, 2)), ("K", (7, 2))):
                if (j, hh) == at:
                    ev.append((name, nxt, 0, 1))
        for after, slot, name in ((2, 3, "ctx_T"), (3, 2, "out_proj"), (4, 3, "x_T")):
            t = self.earlier(i, j, after, main, prev)
            if t and hh == slot and t[2] % 4 == 3:
                ev.append((name,) + t)
        return ev

    def count(self, i, main, nxt, prev):
        return sum(len(self.events(i, j, hh, main, nxt, prev)) for j in range(self.G) for hh in range(4))

    def x_start(self, i):
        if isinstance(i, int):
            return self.x_before[i]
        full = self.x_before[2] - self.x_before[1]
        return i * full + (self.x_before[1] - full)

    def slots_of_step(self, i, main, nxt, prev, only=None):
        x, n = self.x_start(i), 0
        for j in range(self.G):
            for hh in range(4):
                evs = []
                for ev in self.events(i, j, hh, main, nxt, prev):
                    evs.append(ev + (x + n,))
                    n += 1
                if only is None or j == only[0] and hh in only[1]:
                    yield j, hh, evs


def run_steps(eng, first, second, step):
    step(first, -1, False, first, None)
    step(first, 0, True, first, None)
    with eng.Fori(1, first.S - 1) as i:
        step(first, i, True, first, first)
    step(first, first.S - 1, True, second, first)
    step(second, 0, True, second, first)
    with eng.Fori(1, second.S - 2) as i:
        step(second, i, True, second, second)
    step(second, second.S - 2, True, second, second)
    step(second, second.S - 1, True, None, second)


def count_events(first, second, x):
    for ph, other in ((first, None), (second, first)):
        for i in range(-1 if ph is first else 0, ph.S + (ph is second)):
            ph.x_before[i] = x
            nxt = ph if i < ph.S - 1 else second if ph is first else None
            x += ph.count(i, 0 <= i < ph.S, nxt, None if i < 0 else ph if i > 0 else other)
    return x


def run_blocks(eng, block):
    block(0, True, False)
    with eng.Fori(1, BLOCKS) as tb:
        block(tb, True, True)
    block(BLOCKS, False, True)


def wait(eng, sem, value):
    if not isinstance(value, int) or value > 0:
        eng.wait_ge(sem, value)


def decoder_layer(nc, x_tok_d, kvT_d, w_lat_d, w_self_d, w_cross_d, wg_d, w1_d, w2_d, out_d):
    SELF = Phase(0, True, T, 2, 3, 0, 0, 0, 0, 0)
    items, units, banks = B * 4, B * 4 * SELF.UN, B * 4 * SELF.MB
    CROSS = Phase(1, False, TC, 1, 2, items, units, banks, SELF.S, B)
    XN = count_events(SELF, CROSS, 1)
    ALL_UNITS, ALL_BANKS = units + B * 4 * CROSS.UN, banks + B * 4 * CROSS.MB

    ctx = ExitStack()
    with ctx:
        def sb(name, shape, dt=F32):
            return ctx.enter_context(nc.sbuf_tensor(name, shape, dt))

        def pb(name, shape):
            return ctx.enter_context(nc.psum_tensor(name, shape, F32))

        def sem(name):
            return ctx.enter_context(nc.semaphore(name))

        x_tok = sb("x_tok", [P, NT, D])
        xT = sb("xT", [P, B * T])
        kvT = sb("kvT", [P, KV])
        w_self = sb("w_self", [P, 4, D])
        w_cross = sb("w_cross", [P, 4, D])
        w_lat = sb("w_lat", [32, 3, D])
        w_gate = sb("w_gate", [P, E])
        w1 = sb("w1", [P, E, HID])
        w1_hi = sb("w1_hi", [P, E * HID], F32R)
        w1_lo = sb("w1_lo", [P, E * HID], F32R)
        w2 = sb("w2", [P, E, 2, D])
        ident = sb("ident", [P, P])
        ident_b = sb("ident_b", [P, P], BF16)
        mask_b = sb("mask_b", [P, P], BF16)
        k_parts = sb("k_parts", [P, 2, KV], F32R)
        q_parts = sb("q_parts", [P, 2, KV], F32R)
        k_stack = sb("k_stack", [P, 8192], F32R)
        q_stack = sb("q_stack", [P, 8192], F32R)
        probs = sb("probs", [P, 2, 4096])
        v_new = sb("v_new", [P, KV // P, D])
        v_aug = sb("v_aug", [P, KV // P, H, VW])
        mx = sb("mx", [P, 2, QT, 4])
        mx_row = sb("mx_row", [4, 2, T], F32R)
        u_sb = sb("u_sb", [P, T])
        rden = sb("rden", [P, QT, 4])
        ctxn = sb("ctxn", [P, QT, D])
        ctxT = sb("ctxT", [P, T])
        y_sb = sb("y_sb", [P, 4, D])
        xn = sb("xn", [P, QT, D])
        stats = sb("stats", [P, 4, 6])
        mv = sb("mv", [P, 4, 2])
        rstd = sb("rstd", [P, 4])
        minus_half = sb("minus_half", [P, 4])
        lmax = sb("lmax", [P, NT])
        lsub = sb("lsub", [P, NT, E])
        lexp = sb("lexp", [P, NT, E])
        lsum = sb("lsum", [P, NT])
        lrec = sb("lrec", [P, NT])
        gp = sb("gp", [P, NT, 2 * E])
        top = sb("top", [P, NT, E])
        rest = sb("rest", [P, NT, 2 * E])
        comb = sb("comb", [P, NT, E])
        comb_b = sb("comb_b", [P, BT, E])
        acc = sb("acc", [P, 2, BT, D])
        res = sb("res", [P, 4, D])

        x_hi, x_lo = q_stack[:, 0:B * T], q_stack[:, B * T:2 * B * T]
        relu, sq = [probs[:, 0, n:n + 2048].rearrange("p (e c t) -> p e c t", e=2, c=2) for n in (0, 2048)]

        ps_s = pb("ps_s", [P, 2, 1024])
        ps_m = pb("ps_m", [P, 2, 512])
        ps_u = pb("ps_u", [P, 512])
        ps_x = pb("ps_x", [P, 512])

        k_scr = [nc.dram_tensor("k_scr_s", (SELF.S, 4, P, KV), F32).ap(),
                 nc.dram_tensor("k_scr_c", (CROSS.S, 4, P, KV), F32).ap()]
        q_scr = [nc.dram_tensor("q_scr_s", (SELF.S, 4, P, SELF.qcols), F32).ap(),
                 nc.dram_tensor("q_scr_c", (CROSS.S, 4, P, CROSS.qcols), F32).ap()]

        kv_loaded = sem("kv_loaded")
        taken = sem("taken")
        x_loaded = sem("x_loaded")
        lat_loaded = sem("lat_loaded")
        w_loaded, cross_loaded = sem("w_loaded"), sem("cross_loaded")
        w1_loaded, ffn_loaded = sem("w1_loaded"), sem("ffn_loaded")
        init_done = sem("init_done")
        q_stack_zero = sem("q_stack_zero")
        const_done = sem("const_done")
        qk_done = sem("qk_done")
        exp_done = sem("exp_done")
        masked = sem("masked")
        max_done = sem("max_done")
        max_read = sem("max_read")
        q_row_zero = sem("q_row_zero")
        mx_loaded = [sem(f"mx_loaded{p}") for p in range(2)]
        pv_done = sem("pv_done")
        u_read = sem("u_read")
        u_turned, u_divided = sem("u_turned"), sem("u_divided")
        x_full = sem("x_full")
        x_read = sem("x_read")
        k_hi, q_hi = sem("k_hi"), sem("q_hi")
        k_spilled, q_spilled = sem("k_spilled"), sem("q_spilled")
        stack_loaded = [[sem(f"stack{n}_{s}") for s in range(ph.slots)] for n, ph in enumerate((SELF, CROSS))]
        v_spread = sem("v_spread")
        rden_done = sem("rden_done")
        ln_chain = sem("ln_chain")
        mv_ready = sem("mv_ready")
        rstd_chain = sem("rstd_chain")
        x_new = sem("x_new")
        lt_done, lt_sub, lt_exp = sem("lt_done"), sem("lt_sub"), sem("lt_exp")
        gate_chain, comb_ready = sem("gate_chain"), sem("comb_ready")
        ffn_hi, ffn_lo = sem("ffn_hi"), sem("ffn_lo")
        h_done, relu_done = sem("h_done"), sem("relu_done")
        sq_done = [sem("sq_done0"), sem("sq_done1")]
        y_done, acc_chain = sem("y_done"), sem("acc_chain")
        comb_copied = sem("comb_copied")
        fin_chain, fin_mv, fin_rstd = sem("fin_chain"), sem("fin_mv"), sem("fin_rstd")
        fin_done = sem("fin_done")
        stored = sem("stored")

        def apart(eng):
            eng.sem_inc(taken, 1)

        W = {SELF: w_self, CROSS: w_cross}

        def k_view(ph, slot_item, hh):
            n = (4 * slot_item + hh) * ph.keys
            return k_stack[:, n:n + ph.keys]

        def q_view(ph, slot_item, hh, q0=0, q1=T):
            n = (4 * slot_item + hh) * T
            return q_stack[:, n + q0:n + q1]

        block = ctx.enter_context(nc.Block())

        @block.sync
        def _(sp):
            sp.dma_start(w_lat[:, :, :], w_lat_d).then_inc(lat_loaded, 16)
            sp.dma_start(kvT[:, :], kvT_d[0]).then_inc(kv_loaded, 16)
            sp.dma_start(w1[:, :, :], w1_d).then_inc(w1_loaded, 16)

            def step(ph, i, main, nxt, prev, only=None):
                for j, hh, evs in ph.slots_of_step(i, main, nxt, prev, only):
                    for name, eph, ei, arg, x in evs:
                        if name == "max_T":
                            sp.wait_ge(x_read, x + 1)
                            c = (arg % eph.G) * 4 * T
                            sp.dma_start(q_stack[ROW_M:ROW_M + 1, c:c + 4 * T].bitcast(F32),
                                         mx_row[:, arg % 2, :].bitcast(F32)).then_inc(mx_loaded[arg % 2], 16)
                        if name in ("K", "Q"):
                            sp.wait_ge(x_read, x + 1)
                            apart(sp)
                            scr = (k_scr if name == "K" else q_scr)[eph.n][ei + arg]
                            parts, cols = (k_parts, KV) if name == "K" else (q_parts, eph.qcols)
                            order = "(rep hl) p k -> rep p hl k" if name == "K" else "(hl rep) p k -> rep p hl k"
                            dst = scr.rearrange(order, rep=2)
                            for rep in range(2):
                                sp.dma_start(dst[rep], parts[:, :, 0:cols].bitcast(F32))\
                                  .then_inc(k_spilled if name == "K" else q_spilled, 16)
                        if name == "V" and not (eph is CROSS and isinstance(ei, int) and ei + arg == CROSS.S - 1):
                            sp.wait_ge(x_full, x + 1)
                            apart(sp)
                            sp.dma_start(kvT[:, :], kvT_d[ei + (arg + eph.step0 + 1)]).then_inc(kv_loaded, 16)
                    if nxt and (j, hh) in ph.load_at:
                        slot = ph.load_at.index((j, hh))
                        nph, ni = (ph, i + 1) if nxt is ph else (nxt, 0)
                        if main:
                            sp.wait_ge(qk_done, ph.units(i, (slot + 1) * (ph.G // ph.slots)))
                            apart(sp)
                        else:
                            if slot == 0:
                                sp.wait_ge(const_done, 1)
                            sp.wait_ge(q_stack_zero, slot + 1)
                        if slot == 0:
                            sp.wait_ge(k_spilled, (i + (2 + ph.step0)) * 32)
                            sp.wait_ge(q_spilled, (i + (2 + ph.step0)) * 32)
                            apart(sp)
                        for scr, stack, width in ((k_scr, k_stack, nph.keys), (q_scr, q_stack, T)):
                            if nph is SELF:
                                bb, h0 = slot // 2, (slot % 2) * 8
                                cols = 8 * width
                                src = scr[0][ni].rearrange("r (d h) k -> (r d) h k", d=HD)\
                                    [:, h0:h0 + 8, bb * width:(bb + 1) * width]
                            else:
                                cols = 4 * width
                                src = scr[1][ni, :, 32 * slot:32 * slot + 32, :]\
                                    .rearrange("r (d h) k -> r d (h k)", d=HD)
                            sp.dma_start(stack[0:4 * HD, slot * cols:(slot + 1) * cols].bitcast(F32), src)\
                              .then_inc(stack_loaded[nph.n][slot], 16)
                    if ph is SELF and isinstance(i, int) and i == 0 and hh == 2:
                        if j < 4:
                            sp.dma_start(x_tok[:, j * BT:(j + 1) * BT, :], x_v[j]).then_inc(x_loaded, 16)
                        else:
                            e = (j - 4) * 2
                            sp.dma_start(w2[:, e:e + 2, :, :], w2_d[:, e:e + 2, :, :]).then_inc(ffn_loaded, 16)
                        if j == 7:
                            sp.dma_start(w_cross[:, :, :], w_cross_d).then_inc(cross_loaded, 16)
                            sp.dma_start(w_gate[:, :], wg_d).then_inc(ffn_loaded, 16)

            x_v = x_tok_d.rearrange("(b t p) d -> b p t d", t=BT, p=P)
            run_steps(sp, SELF, CROSS, step)
            out_v = out_d.rearrange("(b t p) d -> b p t d", t=4, p=P)
            with sp.Fori(0, 4) as tb:
                sp.wait_ge(fin_done, tb * 4 + 4)
                apart(sp)
                sp.dma_start(out_v[tb], res[:, :, :]).then_inc(stored, 16)
            sp.wait_ge(stored, 16 * 4)

        @block.gpsimd
        def _(pool):
            pool.memset(ident[:, :], 0.0).then_inc(init_done, 1)
            pool.memset(ident_b[:, :], 0.0).then_inc(init_done, 1)
            pool.memset(mask_b[:, :], 0.0).then_inc(init_done, 1)
            pool.memset(k_stack[:, :].bitcast(F32), -1.0).then_inc(init_done, 1)
            pool.memset(v_aug[:, :, :, :].rearrange("p a b c -> p (a b c)"), 0.0).then_inc(init_done, 1)
            pool.wait_ge(init_done, 5)
            for m in (ident, ident_b):
                pool.affine_select(out=m[:, :], in_=m[:, :], compare_op=ALU.not_equal, fill=1.0, base=0,
                                   pattern=[[-1, P]], channel_multiplier=1).then_inc(init_done, 1)
            pool.affine_select(out=mask_b[:, :], in_=mask_b[:, :], compare_op=ALU.is_ge, fill=MASKED, base=0,
                               pattern=[[-1, P]], channel_multiplier=1).then_inc(init_done, 1)
            pool.memset(v_aug[:, :, :, HD:HD + 1].rearrange("p a b c -> p (a b c)"), 1.0).then_inc(init_done, 1)
            pool.memset(gp[:, :, E:2 * E], -1.0).then_inc(init_done, 1)
            pool.memset(minus_half[:, :], -0.5).then_inc(init_done, 1)
            pool.wait_ge(init_done, 11)
            pool.memset(top[:, :, :], -1.0).then_inc(const_done, 1)

            def inv_std(tiles, chain, base):
                apart(pool)
                pool.tensor_scalar(rstd[:, 0:tiles], mv[:, 0:tiles, 1], LN_EPS, 1.0, ALU.add, ALU.mult)\
                    .then_inc(chain, 1)
                pool.wait_ge(chain, base + 1)
                pool.tensor_tensor(rstd[:, 0:tiles], rstd[:, 0:tiles], minus_half[:, 0:tiles], ALU.pow)\
                    .then_inc(chain, 1)
                pool.wait_ge(chain, base + 2)
                apart(pool)

            def step(ph, i, main, nxt, prev, only=None):
                for j in range(ph.G) if only is None else only[:1]:
                    w = ph.item(i, j)
                    if j == 0 and main:
                        pool.wait_ge(x_read, ph.x_start(i))
                        wait(pool, pv_done, w)
                        apart(pool)
                        pool.tensor_scalar(v_aug[:, :, :, 0:HD],
                                           v_new[:, :, :].rearrange("p c (h d) -> p c h d", d=HD),
                                           1.0, 0.0, ALU.mult, ALU.add).then_inc(v_spread, 1)
                        pool.wait_ge(v_spread, i + (ph.step0 + 1))
                    if main and ph.causal:
                        pool.wait_ge(exp_done, ph.units(i, j + 1))
                        apart(pool)
                        pr = probs[:, j % 2, 0:2048].rearrange("p (b q) -> p b q", q=256)[:, :, 0:P]
                        pool.affine_select(out=pr, in_=pr, compare_op=ALU.is_ge, fill=0.0, base=0,
                                           pattern=[[0, 8], [1, P]], channel_multiplier=-1)\
                            .then_inc(masked, 1)
                    last = ph.earlier(i, j, 3, main, prev)
                    if last and last[2] % 4 == 3:
                        bph, bi, bj = last
                        bn = bi * bph.bps + (bph.batch0 + bj // 4)
                        pool.wait_ge(mv_ready, bn * QT + QT)
                        inv_std(QT, rstd_chain, bn * 2)
                    if main:
                        pool.wait_ge(qk_done, ph.units(i, j + 1))
                        apart(pool)
                        if ph.causal:
                            pool.wait_ge(masked, w + 1)
                            apart(pool)
                        c = j * 4 * T
                        pool.memset(q_stack[ROW_M:ROW_M + 1, c:c + 4 * T].bitcast(F32), 0.0).then_inc(q_row_zero, 1)
                        pool.wait_ge(q_row_zero, w + 1)

            run_steps(pool, SELF, CROSS, step)


            def block_(tb, main, prev):
                for e in range(E if main else 2):
                    if main:
                        pool.wait_ge(relu_done, tb * (2 * E) + (2 * e + 1))
                        wait(pool, y_done, tb * E + (e - 1))
                        pool.tensor_tensor(sq[:, e % 2, 0, :], relu[:, e % 2, 0, :], relu[:, e % 2, 0, :],
                                           ALU.mult).then_inc(sq_done[0], 1)
                    if e == 1 and prev:
                        pool.wait_ge(fin_mv, tb * BT)
                        inv_std(BT, fin_rstd, tb * 2 - 2)
                    if isinstance(tb, int) and main and e == 5:
                        step(CROSS, CROSS.S, False, None, CROSS, REST_AT[4])

            run_blocks(pool, block_)

        @block.scalar
        def _(act):
            def copy(out, in_):
                return nc.scalar.activation(out, in_, ACT.Copy)

            act.dma_start(w_self[:, 0::3, :], w_self_d).then_inc(w_loaded, 16)
            act.wait_ge(x_full, 1)
            copy(w_self[:, 1:3, :].rearrange("p a b -> p (a b)"), ps_x[:, 0:2 * D]).then_inc(x_read, 1)

            def split_w1():
                act.wait_ge(w1_loaded, 16)
                copy(w1_hi[:, :], w1[:, :, :].rearrange("p e n -> p (e n)")).then_inc(ffn_hi, 1)

            def gate_exp(part):
                t0, t1 = GATE_TILES[part]
                act.wait_ge(lt_sub, part + 1)
                nc.scalar.activation(lexp[:, t0:t1, :], lsub[:, t0:t1, :], ACT.Exp).then_inc(lt_exp, 1)

            def begin_ffn(at):
                if at == (1, 3):
                    act.wait_ge(k_spilled, 32 * (SELF.S + CROSS.S))
                    copy(k_parts[:, 0, :], xT[:, 0:KV]).then_inc(ffn_hi, 1)

            def step(ph, i, main, nxt, prev, only=None):
                for j, hh, evs in ph.slots_of_step(i, main, nxt, prev, only):
                    w = ph.item(i, j)
                    if main and hh % ph.UH == 0:
                        u = hh // ph.UH
                        act.wait_ge(qk_done, ph.units(i, j) + (u + 1))
                        if hh == 0:
                            wait(act, pv_done, w - 1)
                        if ph.causal:
                            nc.scalar.activation(
                                probs[:, j % 2, u * 1024:u * 1024 + 1024]
                                .rearrange("p (h c) -> p h c", h=2)[:, :, 0:384],
                                ps_s[:, u % 2, :].rearrange("p (h c) -> p h c", h=2)[:, :, 0:384],
                                ACT.Exp, scale=SCALE).then_inc(exp_done, 1)
                        else:
                            nc.scalar.activation(probs[:, j % 2, hh * 1024:hh * 1024 + 1024], ps_s[:, u % 2, :],
                                                 ACT.Exp, scale=SCALE).then_inc(exp_done, 1)
                    if hh == 3 and ph.earlier(i, j, 1, main, prev):
                        act.wait_ge(pv_done, w)
                        wait(act, u_turned, w - 1)
                        copy(u_sb[:, :], ps_u[:, 0:T]).then_inc(u_read, 1)
                    for name, eph, ei, arg, x in evs:
                        if name in ("max_T", "K", "Q", "V", "ctx_T", "x_T"):
                            act.wait_ge(x_full, x + 1)
                        if name == "max_T":
                            copy(mx_row[:, arg % 2, :], ps_x[0:4, 0:T]).then_inc(x_read, 1)
                        if name == "K":
                            wait(act, k_spilled, ei * 32 + 32 * (arg + eph.step0))
                            copy(k_parts[:, 0, :], ps_x[:, 0:KV]).then_inc(k_hi, 1)
                        if name == "Q":
                            wait(act, q_spilled, ei * 32 + 32 * (arg + eph.step0))
                            copy(q_parts[:, 0, 0:eph.qcols], ps_x[:, 0:eph.qcols]).then_inc(q_hi, 1)
                        if name == "V":
                            wait(act, v_spread, ei + (arg + eph.step0))
                            copy(v_new[:, :, :].rearrange("p c n -> p (c n)"), ps_x[:, 0:KV]).then_inc(x_read, 1)
                        if name == "ctx_T":
                            copy(ctxT[:, :], ps_x[:, 0:T]).then_inc(x_read, 1)
                        if name == "x_T":
                            b = ei * eph.bps + arg // 4
                            copy(x_tok[:, bass.ds(b * QT, QT), :], xn[:, :, :])
                            copy(xT[:, bass.ds(b * T, T)], ps_x[:, 0:T]).then_inc(x_read, 1)
                    if isinstance(i, int) and i < 0 and (j, hh) == ph.at["V"]:
                        split_w1()
                    if ph is CROSS and isinstance(i, int) and i == CROSS.S - 1:
                        begin_ffn((j, hh))

            run_steps(act, SELF, CROSS, step)

            act.wait_ge(max_done, ALL_BANKS)
            act.wait_ge(q_row_zero, 2 * items)

            def block_(tb, main, prev):
                for e in range(E if main else 0):
                    for c in range(2):
                        act.wait_ge(h_done, tb * (2 * E) + (2 * e + c + 1))
                        wait(act, sq_done[c], tb * E + (e - 1))
                        nc.scalar.activation(relu[:, e % 2, c, :], ps_s[:, e % 2, 512 * c:512 * c + 512],
                                             ACT.Relu).then_inc(relu_done, 1)
                    if isinstance(tb, int) and main and e in REST_AT:
                        step(CROSS, CROSS.S, False, None, CROSS, REST_AT[e])
                    if isinstance(tb, int) and e in (2, 7):
                        c0, c1 = (512, 1536) if e == 2 else (1536, 2048)
                        if e == 7:
                            act.wait_ge(x_read, XN)
                        copy(x_hi[:, c0:c1], xT[:, c0:c1]).then_inc(ffn_hi, 1)
                    if isinstance(tb, int) and e in (0, 7):
                        gate_exp(e // 7)

            run_blocks(act, block_)

        @block.vector
        def _(dve):
            v = nc.vector

            def clear(slots):
                for slot in slots:
                    v.memset(q_stack[:, slot * 2048:(slot + 1) * 2048].bitcast(F32), 0.0).then_inc(q_stack_zero, 1)

            clear((0, 1))
            def bn_stats(y, tiles, done):
                for t in range(tiles):
                    v.bn_stats(stats[:, t, :], y[:, t, :]).then_inc(done, 1)

            def bn_aggr(tiles, done):
                apart(dve)
                for t in range(tiles):
                    v.bn_aggr(mv[:, t, :], stats[:, t, :]).then_inc(done, 1)

            def normalise(y, out, tiles, done):
                apart(dve)
                for t in range(tiles):
                    v.tensor_scalar(out[:, t, :], y[:, t, :], mv[:, t, 0:1], rstd[:, t:t + 1],
                                    ALU.subtract, ALU.mult).then_inc(done, 1)

            def divide(w, item):
                dve.wait_ge(u_turned, w - 1)
                g = item[2] % 4
                u = ps_u[:, T:2 * T].rearrange("p (t h c) -> p t h c", t=QT, c=VW)
                v.reciprocal(rden[:, :, :], u[:, :, :, HD]).then_inc(rden_done, 1)
                dve.wait_ge(rden_done, w - 1)
                o = ctxn[:, :, 32 * g:32 * g + 32].rearrange("p t (h c) -> p t h c", c=HD)
                v.tensor_tensor(o, u[:, :, :, 0:HD], rden[:, :, :, None].broadcast_to([P, QT, 4, HD]),
                                ALU.mult).then_inc(u_divided, 1)

            def split_w1():
                dve.wait_ge(ffn_hi, 1)
                v.tensor_tensor(w1_lo[:, :], w1[:, :, :].rearrange("p e n -> p (e n)"),
                                w1_hi[:, :].bitcast(F32), ALU.subtract).then_inc(ffn_lo, 1)

            def gate(part):
                t0, t1 = GATE_TILES[part]
                n = t1 - t0
                count = 8 * part + 2 * t0

                def link(ins, more=0):
                    nonlocal count
                    count += 1 + more
                    ins.then_inc(gate_chain, 1)
                    dve.wait_ge(gate_chain, count)
                    apart(dve)

                dve.wait_ge(lt_done, part + 1)
                lt = (ps_m[:, 0, 0:n * E] if part == 0 else ps_u[:, 0:n * E]).rearrange("p (t e) -> p t e", e=E)
                link(v.tensor_reduce(out=lmax[:, t0:t1], in_=lt, axis=AX.X, op=ALU.max))
                v.tensor_tensor(lsub[:, t0:t1, :], lt, lmax[:, t0:t1, None].broadcast_to([P, n, E]),
                                ALU.subtract).then_inc(lt_sub, 1)
                dve.wait_ge(lt_exp, part + 1)
                link(v.tensor_reduce(out=lsum[:, t0:t1], in_=lexp[:, t0:t1, :], axis=AX.X, op=ALU.add))
                link(v.reciprocal(lrec[:, t0:t1], lsum[:, t0:t1]))
                link(v.tensor_tensor(gp[:, t0:t1, 0:E], lexp[:, t0:t1, :],
                                     lrec[:, t0:t1, None].broadcast_to([P, n, E]), ALU.mult))
                for t in range(t0, t1 - 1):
                    v.max(out=rest[:, t, 0:E], in_=gp[:, t, 0:E]).then_inc(gate_chain, 1)
                link(v.max(out=rest[:, t1 - 1, 0:E], in_=gp[:, t1 - 1, 0:E]), n - 1)
                link(v.tensor_copy(top[:, t0:t1, 0:2], rest[:, t0:t1, 0:2]))
                link(v.scalar_tensor_tensor(lsum[:, t0:t1], top[:, t0:t1, 0], TOPW_EPS, top[:, t0:t1, 1],
                                            op0=ALU.add, op1=ALU.add))
                v.reciprocal(lrec[:, t0:t1], lsum[:, t0:t1]).then_inc(gate_chain, 1)
                for t in range(t0, t1 - 1):
                    v.match_replace(out=rest[:, t, :], in_to_replace=top[:, t, :], in_values=gp[:, t, :],
                                    imm_value=0.0).then_inc(gate_chain, 1)
                link(v.match_replace(out=rest[:, t1 - 1, :], in_to_replace=top[:, t1 - 1, :],
                                     in_values=gp[:, t1 - 1, :], imm_value=0.0), n)
                link(v.tensor_tensor(comb[:, t0:t1, :], gp[:, t0:t1, 0:E], rest[:, t0:t1, 0:E], ALU.subtract))
                v.tensor_tensor(comb[:, t0:t1, :], comb[:, t0:t1, :],
                                lrec[:, t0:t1, None].broadcast_to([P, n, E]), ALU.mult).then_inc(comb_ready, 1)

            def begin_ffn(at):
                if at == (1, 3):
                    dve.wait_ge(ffn_hi, 2)
                    v.tensor_tensor(k_parts[:, 1, :], xT[:, 0:KV], k_parts[:, 0, :].bitcast(F32),
                                    ALU.subtract).then_inc(ffn_lo, 1)

            def step(ph, i, main, nxt, prev, only=None):
                for j, hh, evs in ph.slots_of_step(i, main, nxt, prev, only):
                    w = ph.item(i, j)
                    t_item = ph.later(i, j, 0, main, nxt)
                    if t_item:
                        tph, ti, tj = t_item
                        if tph.causal:
                            dve.wait_ge(max_done, tph.banks(ti, tj) + (hh + 1))
                            v.tensor_reduce(out=mx[:, tj % 2, 0, hh:hh + 1], in_=ps_m[:, hh % 2, 0:P],
                                            axis=AX.X, op=ALU.max)
                            v.tensor_reduce(out=mx[:, tj % 2, 1, hh:hh + 1], in_=ps_m[:, hh % 2, P:3 * P],
                                            axis=AX.X, op=ALU.max).then_inc(max_read, 1)
                        else:
                            dve.wait_ge(max_done, tph.banks(ti, tj) + (2 * hh + 1))
                            v.tensor_reduce(out=mx[:, tj % 2, 0, hh:hh + 1], in_=ps_m[:, 0, :],
                                            axis=AX.X, op=ALU.max).then_inc(max_read, 1)
                    two_ago = ph.earlier(i, j, 2, main, prev)
                    if hh == 0 and two_ago:
                        divide(w, two_ago)
                    if t_item and not tph.causal:
                        dve.wait_ge(max_done, tph.banks(ti, tj) + (2 * hh + 2))
                        v.tensor_reduce(out=mx[:, tj % 2, 1, hh:hh + 1], in_=ps_m[:, 1, :],
                                        axis=AX.X, op=ALU.max).then_inc(max_read, 1)
                    last = ph.earlier(i, j, 3, main, prev)
                    if hh == 3 and last and last[2] % 4 == 3:
                        dve.wait_ge(x_read, added)
                        bn_stats(y_sb, QT, ln_chain)
                    last = ph.earlier(i, j, 4, main, prev)
                    if hh == 0 and last and last[2] % 4 == 3:
                        bph, bi, bj = last
                        dve.wait_ge(ln_chain, bi * (QT * bph.bps) + QT * (bph.batch0 + bj // 4 + 1))
                        bn_aggr(QT, mv_ready)
                    if hh == 2 and last and last[2] % 4 == 3:
                        bph, bi, bj = last
                        dve.wait_ge(rstd_chain, bi * (2 * bph.bps) + 2 * (bph.batch0 + bj // 4 + 1))
                        normalise(y_sb, xn, QT, x_new)
                    for name, eph, ei, arg, x in evs:
                        if name in ("K", "Q"):
                            dve.wait_ge(k_hi if name == "K" else q_hi, ei + (arg + eph.step0 + 1))
                            parts, cols = (k_parts, KV) if name == "K" else (q_parts, eph.qcols)
                            v.tensor_tensor(parts[:, 1, 0:cols], ps_x[:, 0:cols],
                                            parts[:, 0, 0:cols].bitcast(F32), ALU.subtract).then_inc(x_read, 1)
                        if name == "out_proj":
                            dve.wait_ge(x_full, x + 1)
                            b = ei * eph.bps + arg // 4
                            if eph is SELF and isinstance(ei, int) and ei == 0:
                                dve.wait_ge(x_loaded, 16 * BLOCKS)
                            bn = ei * eph.bps + (eph.batch0 + arg // 4)
                            wait(dve, x_new, bn * QT)
                            v.tensor_tensor(y_sb[:, 0:QT, :],
                                            ps_x[:, 0:T].rearrange("p (t d) -> p t d", t=QT),
                                            x_tok[:, bass.ds(b * QT, QT), :], ALU.add).then_inc(x_read, 1)
                            added = x + 1
                    if isinstance(i, int) and i < 0 and (j, hh) == ph.at["Q"]:
                        clear((2, 3))
                    if isinstance(i, int) and i < 0 and (j, hh) == ph.at["V"]:
                        split_w1()
                    if ph is CROSS and isinstance(i, int) and i == CROSS.S - 1:
                        begin_ffn((j, hh))

            run_steps(dve, SELF, CROSS, step)

            def block_(tb, main, prev):
                for e in range(E if main else 2):
                    if isinstance(tb, int) and main and e in (0, 6):
                        step(CROSS, CROSS.S, False, None, CROSS, REST_AT[e])
                    if main:
                        dve.wait_ge(relu_done, tb * (2 * E) + (2 * e + 2))
                        wait(dve, y_done, tb * E + (e - 1))
                        v.tensor_tensor(sq[:, e % 2, 1, :], relu[:, e % 2, 1, :], relu[:, e % 2, 1, :],
                                        ALU.mult).then_inc(sq_done[1], 1)
                    if isinstance(tb, int) and main and e == 0:
                        gate(0)
                    if main if e > 1 else prev:
                        ex, a = (e - 2) % E, e % 2
                        n = tb * E + (e - 2)
                        if ex == 0:
                            wait(dve, acc_chain, n * BT)
                            if isinstance(tb, int) and tb == 0:
                                dve.wait_ge(comb_ready, 1)
                            dve_copy = v.tensor_copy(comb_b[:, :, :], comb[:, bass.ds(tb * BT, BT), :])
                            dve_copy.then_inc(comb_copied, 1)
                            dve.wait_ge(comb_copied, tb + 1)
                            apart(dve)
                        else:
                            dve.wait_ge(acc_chain, n * BT)
                            if ex == 1:
                                wait(dve, fin_done, tb * BT)
                            apart(dve)
                        dve.wait_ge(y_done, n + 1)
                        for t in range(BT):
                            src = x_tok[:, bass.ds(tb * BT + t, 1), :].rearrange("p a d -> p (a d)") if ex == 0 \
                                else acc[:, 1 - a, t, :]
                            v.scalar_tensor_tensor(acc[:, a, t, :], ps_m[:, a, t * D:(t + 1) * D],
                                                   comb_b[:, t, ex:ex + 1], src, op0=ALU.mult, op1=ALU.add)\
                                .then_inc(acc_chain, 1)
                    if e == 1 and prev:
                        dve.wait_ge(acc_chain, tb * (BT * E))
                        bn_stats(acc[:, 1], BT, fin_chain)
                        dve.wait_ge(fin_chain, tb * BT)
                        bn_aggr(BT, fin_mv)
                    if prev and e == (2 if main else 1):
                        dve.wait_ge(fin_rstd, tb * 2)
                        wait(dve, stored, tb * 16 - 16)
                        normalise(acc[:, 1], res, BT, fin_done)
                    if isinstance(tb, int) and main and e in (1, 3, 4, 5):
                        step(CROSS, CROSS.S, False, None, CROSS, REST_AT[e])
                    if isinstance(tb, int) and main and e in (2, 7):
                        c0, c1 = (512, 1536) if e == 2 else (1536, 2048)
                        dve.wait_ge(ffn_hi, 3 if e == 2 else 4)
                        v.tensor_tensor(x_lo[:, c0:c1], xT[:, c0:c1], x_hi[:, c0:c1].bitcast(F32),
                                        ALU.subtract).then_inc(ffn_lo, 1)
                    if isinstance(tb, int) and main and e == 7:
                        gate(1)

            run_blocks(dve, block_)

        @block.tensor
        def _(pe):
            mm = nc.tensor.matmul
            pe.wait_ge(lat_loaded, 16)
            for n in range(2):
                last = mm(ps_x[:, n * D:(n + 1) * D], w_lat[:, 0, :], w_lat[:, 1 + n, :], start=True, stop=True)
            last.then_inc(x_full, 1)

            def logits(part, out):
                t0, t1 = GATE_TILES[part]
                for t in range(t0, t1):
                    last = mm(out[:, (t - t0) * E:(t - t0 + 1) * E], xT[:, t * P:(t + 1) * P], w_gate[:, :],
                              start=True, stop=True)
                last.then_inc(lt_done, 1)

            def step(ph, i, main, nxt, prev, only=None):
                for j, hh, evs in ph.slots_of_step(i, main, nxt, prev, only):
                    w = ph.item(i, j)
                    if main and hh % ph.UH == 0:
                        u = hh // ph.UH
                        if hh == 0:
                            pe.wait_ge(mx_loaded[j % 2], i * (8 * ph.G) + 16 * ((ph.item0 + j) // 2 + 1))
                        wait(pe, exp_done, ph.units(i, j) + (u - 1))
                        for h in range(hh, hh + ph.UH):
                            for c in range(ph.KC):
                                q0 = c * P if ph.causal else 0
                                col = (h - hh) * 512 + c * T
                                last = mm(ps_s[:, u % 2, col:col + T - q0],
                                          k_view(ph, j, h)[:, c * P:(c + 1) * P], q_view(ph, j, h, q0, T),
                                          start=True, stop=True)
                        last.then_inc(qk_done, 1)
                    t_item = ph.later(i, j, 0, main, nxt)
                    if t_item:
                        tph, ti, tj = t_item
                        local = tj % tph.G
                        if isinstance(i, int) and i < 0 and hh == 0:
                            pe.wait_ge(const_done, 1)
                        if hh == 0:
                            pe.wait_ge(stack_loaded[tph.n][local // (tph.G // tph.slots)],
                                       ti * 32 + 32 * (tj // tph.G + 1))
                            before = SELF.G if isinstance(ti, int) and ti + tj // tph.G == 0 else tph.G
                            wait(pe, q_row_zero, tph.item(ti, tj) + (1 - before))
                        kv = k_view(tph, local, hh)
                        if tph.causal:
                            wait(pe, max_read, tph.banks(ti, tj) + (hh - 1))
                            m = ps_m[:, hh % 2, 0:512].rearrange("p (b q) -> p b q", q=256)[:, :, 0:P]
                            mm(ps_m[:, hh % 2, 0:P], q_view(tph, local, hh, 0, P), kv[:, 0:P],
                               start=True, stop=False)
                            mm(ps_m[:, hh % 2, P:3 * P], q_view(tph, local, hh, P, T), kv, start=False, stop=False)
                            mm(m, ident_b[:, :], mask_b[:, None, :].broadcast_to([P, 2, P]),
                               start=False, stop=True).then_inc(max_done, 1)
                        else:
                            wait(pe, max_read, tph.banks(ti, tj) + (2 * hh - 1))
                            mm(ps_m[:, 0, :], q_view(tph, local, hh, 0, P), kv,
                               start=True, stop=True).then_inc(max_done, 1)
                    if hh == 0 and ph.earlier(i, j, 2, main, prev):
                        pe.wait_ge(u_read, w - 1)
                        for t in range(QT):
                            last = nc.tensor.transpose(ps_u[:, T + t * P:T + (t + 1) * P],
                                                       u_sb[:, t * P:(t + 1) * P], ident[:, :])
                        last.then_inc(u_turned, 1)
                    done = ph.earlier(i, j, 1, main, prev)
                    if done:
                        pph, pi, pj = done
                        chunks = pph.pv_chunks[hh]
                        if 0 in chunks:
                            if pph.causal:
                                pe.wait_ge(masked, w)
                            else:
                                pe.wait_ge(exp_done, pph.units(pi, pj + 1))
                            pe.wait_ge(v_spread, pi + (pph.step0 + pj // pph.G + 1))
                            wait(pe, u_read, w - 1)
                            wait(pe, u_divided, w - 1)
                        for c in chunks:
                            g, c0 = pj % 4, (pj % pph.G // 4) * pph.KC
                            for h in range(4):
                                q0 = c * P if pph.causal else 0
                                col = h * (512 if pph.causal else 1024) + c * T
                                last = mm(ps_u[32 * h:32 * h + 32, q0:T], v_aug[:, c0 + c, 4 * g + h, :],
                                          probs[:, pj % 2, col:col + T - q0],
                                          start=(c == 0), stop=(c == pph.KC - 1))
                        if hh == 3:
                            last.then_inc(pv_done, 1)
                    if t_item and not tph.causal:
                        wait(pe, max_read, tph.banks(ti, tj) + 2 * hh)
                        mm(ps_m[:, 1, :], q_view(tph, local, hh, P, T), kv,
                           start=True, stop=True).then_inc(max_done, 1)
                    for name, eph, ei, arg, x in evs:
                        wait(pe, x_read, x)
                        if name == "max_T":
                            pe.wait_ge(max_read, eph.banks(ei, arg + 1))
                            for t in range(QT):
                                last = nc.tensor.transpose(ps_x[0:4, t * P:(t + 1) * P], mx[:, arg % 2, t, :],
                                                           ident[:, :])
                        if name == "K":
                            if eph is CROSS and isinstance(ei, int) and ei + arg == 0:
                                pe.wait_ge(cross_loaded, 16)
                            pe.wait_ge(kv_loaded, ei * 16 + 16 * (arg + eph.step0 + 1))
                            last = mm(ps_x[:, 0:KV], W[eph][:, 1, :], kvT[:, :], start=True, stop=True)
                        if name == "Q":
                            if eph is SELF:
                                if isinstance(ei, int) and ei < 0:
                                    pe.wait_ge(w_loaded, 16)
                                src = kvT[:, :]
                            elif isinstance(ei, int):
                                src = xT[:, (ei + arg) * T:(ei + arg + 1) * T]
                            else:
                                src = xT[:, bass.ds((ei + arg) * T, T)]
                            last = mm(ps_x[:, 0:eph.qcols], W[eph][:, 0, :], src, start=True, stop=True)
                        if name == "V":
                            for c in range(KV // P):
                                last = mm(ps_x[:, c * D:(c + 1) * D], kvT[:, c * P:(c + 1) * P], W[eph][:, 2, :],
                                          start=True, stop=True)
                        if name == "ctx_T":
                            pe.wait_ge(u_divided, eph.item(ei, arg) + 1)
                            for t in range(QT):
                                last = nc.tensor.transpose(ps_x[:, t * P:(t + 1) * P], ctxn[:, t, :], ident[:, :])
                        if name == "out_proj":
                            for t in range(QT):
                                last = mm(ps_x[:, t * D:(t + 1) * D], ctxT[:, t * P:(t + 1) * P], W[eph][:, 3, :],
                                          start=True, stop=True)
                        if name == "x_T":
                            pe.wait_ge(x_new, ei * (QT * eph.bps) + QT * (eph.batch0 + arg // 4 + 1))
                            for t in range(QT):
                                last = nc.tensor.transpose(ps_x[:, t * P:(t + 1) * P], xn[:, t, :], ident[:, :])
                        last.then_inc(x_full, 1)
                    if ph is CROSS and isinstance(i, int) and i == CROSS.S - 1 and (j, hh) == (2, 3):
                        pe.wait_ge(ffn_loaded, 16 * 5)
                        pe.wait_ge(x_read, CROSS.x_before[CROSS.S - 1])
                        pe.wait_ge(max_read, ALL_BANKS)
                        logits(0, ps_m[:, 0, :])

            run_steps(pe, SELF, CROSS, step)

            pe.wait_ge(exp_done, ALL_UNITS)

            def block_(tb, main, prev):
                for e in range(E if main else 2):
                    if main and prev and e == 2:
                        pe.wait_ge(ffn_lo, 4)
                    if main:
                        for c in range(2):
                            if isinstance(tb, int):
                                toks_hi, toks_lo = k_parts[:, 0, :], k_parts[:, 1, :]
                                if (e, c) == (0, 0):
                                    pe.wait_ge(ffn_lo, 2)
                            else:
                                toks_hi, toks_lo = (x[:, bass.ds(tb * 512, 512)] for x in (x_hi, x_lo))
                            wait(pe, relu_done, tb * (2 * E) + (2 * e + c - 3))
                            w = slice(e * HID + c * P, e * HID + (c + 1) * P)
                            h = ps_s[:, e % 2, 512 * c:512 * c + 512]
                            mm(h, w1_hi[:, w], toks_hi, start=True, stop=False)
                            mm(h, w1_hi[:, w], toks_lo, start=False, stop=False)
                            mm(h, w1_lo[:, w], toks_hi, start=False, stop=True).then_inc(h_done, 1)
                    if main if e > 1 else prev:
                        ex, a = (e - 2) % E, e % 2
                        n = tb * E + (e - 2)
                        if isinstance(tb, int) and (tb, e) == (0, 2):
                            pe.wait_ge(lt_sub, 1)
                        wait(pe, acc_chain, n * BT - BT)
                        pe.wait_ge(sq_done[0], n + 1)
                        pe.wait_ge(sq_done[1], n + 1)
                        for t in range(BT):
                            for c in range(2):
                                last = mm(ps_m[:, a, t * D:(t + 1) * D], sq[:, a, c, t * P:(t + 1) * P],
                                          w2[:, ex, c, :], start=(c == 0), stop=(c == 1))
                        last.then_inc(y_done, 1)
                    if isinstance(tb, int) and main and e in REST_AT:
                        step(CROSS, CROSS.S, False, None, CROSS, REST_AT[e])
                    if isinstance(tb, int) and main and e == 7:
                        pe.wait_ge(x_read, XN)
                        pe.wait_ge(u_divided, 2 * items)
                        logits(1, ps_u[:, :])
                    if isinstance(tb, int) and main and e == E - 1:
                        pe.wait_ge(ffn_lo, 3)

            run_blocks(pe, block_)


def kernel(x, ctx_1024, L0_attn_W_DKV, L0_attn_W_UK, L0_attn_W_UV, L0_attn_W_UQ, L0_attn_W_O,
           L0_xattn_w_q, L0_xattn_w_k, L0_xattn_w_v, L0_xattn_w_o, L0_ffn_Wg, L0_ffn_W1, L0_ffn_W2):
    import numpy as np
    import concourse.bacc as bacc
    from concourse.bass_utils import run_bass_kernel_spmd

    a = {n: np.asarray(v) for n, v in locals().items() if n[0] in "xcL"}
    x, ctx_kv = a["x"], a["ctx_1024"]
    by_dim = np.arange(D).reshape(H, HD).T.reshape(-1)
    by_group = np.arange(D).reshape(4, 4, HD).transpose(0, 2, 1).reshape(-1)
    kvT = np.concatenate([x.reshape(B // 2, KV, D).transpose(0, 2, 1), ctx_kv.transpose(0, 2, 1)])
    arrays = {
        "x_tok": x.reshape(B * T, D),
        "kvT": kvT,
        "w_lat": np.stack([a["L0_attn_W_DKV"].T, a["L0_attn_W_UK"][:, by_dim], a["L0_attn_W_UV"]], axis=1),
        "w_self": np.stack([a["L0_attn_W_UQ"][:, by_dim], a["L0_attn_W_O"]], axis=1),
        "w_cross": np.stack([a["L0_xattn_w_q"].T[:, by_group], a["L0_xattn_w_k"].T[:, by_group],
                             a["L0_xattn_w_v"].T, a["L0_xattn_w_o"].T], axis=1),
        "wg": a["L0_ffn_Wg"],
        "w1": a["L0_ffn_W1"].transpose(1, 0, 2),
        "w2": a["L0_ffn_W2"].reshape(E, 2, P, D).transpose(2, 0, 1, 3),
    }
    arrays = {f"{n}_dram": np.ascontiguousarray(v) for n, v in arrays.items()}
    nc = bacc.Bacc("TRN2", target_bir_lowering=False, num_devices=1)
    args = [nc.dram_tensor(n, v.shape, mybir.dt.from_np(v.dtype), kind="ExternalInput").ap()
            for n, v in arrays.items()]
    out = nc.dram_tensor("out_dram", (B * T, D), F32, kind="ExternalOutput").ap()
    decoder_layer(nc, *args, out)
    r = run_bass_kernel_spmd(nc, [arrays], core_ids=[0])
    return r.results[0]["out_dram"].reshape(B, T, D)
```
